# Optimizing a Trainium2 kernel written in Bass

```python
import numpy as np
import jax
import jax.numpy as jnp

def _softmax(x, axis=-1):
    return jax.nn.softmax(x, axis=axis)

def _gelu(x):
    return jax.nn.gelu(x, approximate=True)

def _silu(x):
    return jax.nn.silu(x)

def _sigmoid(x):
    return jax.nn.sigmoid(x)

def _layernorm(x, axis=-1, eps=1e-05):
    m = jnp.mean(x, axis=axis, keepdims=True)
    v = jnp.var(x, axis=axis, keepdims=True)
    return (x - m) / jnp.sqrt(v + eps)

def _scatter_add(tgt, idx, src, axis=0):
    return tgt.at[idx].add(src)

def _segment_sum(src, seg, n):
    return jax.ops.segment_sum(src, seg, n)
kernel_name = 'mk_cond_seq_d1_seqx_r4_358bfd'

def setup_inputs(seed: int=0):
    np.random.seed(seed)
    _w = jnp.asarray

    def _rec_inputs():
        import jax
        import jax.numpy as jnp
        _rk = jax.random.key(seed)
        x = -0.0003929 + 0.9999 * jax.random.normal(jax.random.fold_in(_rk, 1), (64, 64, 256), jnp.float32)
        _lenS = 64 - jax.random.randint(jax.random.fold_in(_rk, 7), (64,), 0, max(1, 64 // 4) + 1, jnp.int32)
        _lenS2 = 64 - jax.random.randint(jax.random.fold_in(_rk, 8), (64,), 0, max(1, 64 // 4) + 1, jnp.int32)
        cond_1024 = 0.00782532 + 1.00527 * jax.random.normal(jax.random.fold_in(_rk, 11), (64, 256), jnp.float32)
        _validS = jnp.arange(64)[None, :] < _lenS[:, None]
        _validS2 = jnp.arange(64)[None, :] < _lenS2[:, None]
        _causal = jnp.tril(jnp.ones((64, 64), dtype=bool))
        mask_BxS_bk0 = jnp.logical_not(jnp.broadcast_to(_validS[:, :], (64, 64)))
        return (x, cond_1024, mask_BxS_bk0)
    x, cond_1024, mask_BxS_bk0 = _rec_inputs()

    def _L0_cond_setup():
        import jax, jax.numpy as jnp
        import numpy as np
        B, L, D = (8, 512, 256)
        FF_MULT = 2
        EPS = 1e-06

        def _layernorm(x):
            mu = jnp.mean(x, axis=-1, keepdims=True)
            var = jnp.mean(jnp.square(x - mu), axis=-1, keepdims=True)
            return (x - mu) / jnp.sqrt(var + EPS)

        def _ssm_fallback(u, w1, b1, w2, b2):
            h = jax.nn.gelu(u @ w1 + b1, approximate=False)
            return h @ w2 + b2
        key = jax.random.key(seed)
        ks = jax.random.split(key, 20)
        s = 0.02
        inp = {'x': jax.random.normal(ks[0], (B, L, D), jnp.float32), 't': jax.random.normal(ks[1], (B, D), jnp.float32), 'mask': jax.random.randint(ks[2], (B, L), 0, 2) > 0, 'ada_w': jax.random.normal(ks[3], (D, 3 * D), jnp.float32) * s, 'ada_b': jnp.zeros((3 * D,), jnp.float32), 'ssm_w1': jax.random.normal(ks[4], (D, D), jnp.float32) * s, 'ssm_b1': jnp.zeros((D,), jnp.float32), 'ssm_w2': jax.random.normal(ks[5], (D, D), jnp.float32) * s, 'ssm_b2': jnp.zeros((D,), jnp.float32), 'bwd_w1': jax.random.normal(ks[6], (D, D), jnp.float32) * s, 'bwd_b1': jnp.zeros((D,), jnp.float32), 'bwd_w2': jax.random.normal(ks[7], (D, D), jnp.float32) * s, 'bwd_b2': jnp.zeros((D,), jnp.float32), 'ffada_w': jax.random.normal(ks[8], (D, 3 * D), jnp.float32) * s, 'ffada_b': jnp.zeros((3 * D,), jnp.float32), 'ff_w1': jax.random.normal(ks[9], (D, FF_MULT * D), jnp.float32) * s, 'ff_b1': jnp.zeros((FF_MULT * D,), jnp.float32), 'ff_w2': jax.random.normal(ks[10], (FF_MULT * D, D), jnp.float32) * s, 'ff_b2': jnp.zeros((D,), jnp.float32)}
        return inp
    _L0_cond_all = _L0_cond_setup()
    _L0_cond_in = {k: v for k, v in _L0_cond_all.items() if k in ('ada_w', 'ada_b', 'ssm_w1', 'ssm_b1', 'ssm_w2', 'ssm_b2', 'bwd_w1', 'bwd_b1', 'bwd_w2', 'bwd_b2', 'ffada_w', 'ffada_b', 'ff_w1', 'ff_b1', 'ff_w2', 'ff_b2')}
    del _L0_cond_all
    return {'x': x, 'cond_1024': cond_1024, 'mask_BxS_bk0': mask_BxS_bk0, 'L0_cond_ada_w': _L0_cond_in['ada_w'], 'L0_cond_ada_b': _L0_cond_in['ada_b'], 'L0_cond_ssm_w1': _L0_cond_in['ssm_w1'], 'L0_cond_ssm_b1': _L0_cond_in['ssm_b1'], 'L0_cond_ssm_w2': _L0_cond_in['ssm_w2'], 'L0_cond_ssm_b2': _L0_cond_in['ssm_b2'], 'L0_cond_bwd_w1': _L0_cond_in['bwd_w1'], 'L0_cond_bwd_b1': _L0_cond_in['bwd_b1'], 'L0_cond_bwd_w2': _L0_cond_in['bwd_w2'], 'L0_cond_bwd_b2': _L0_cond_in['bwd_b2'], 'L0_cond_ffada_w': _L0_cond_in['ffada_w'], 'L0_cond_ffada_b': _L0_cond_in['ffada_b'], 'L0_cond_ff_w1': _L0_cond_in['ff_w1'], 'L0_cond_ff_b1': _L0_cond_in['ff_b1'], 'L0_cond_ff_w2': _L0_cond_in['ff_w2'], 'L0_cond_ff_b2': _L0_cond_in['ff_b2']}

def reference(x, cond_1024, mask_BxS_bk0, L0_cond_ada_w, L0_cond_ada_b, L0_cond_ssm_w1, L0_cond_ssm_b1, L0_cond_ssm_w2, L0_cond_ssm_b2, L0_cond_bwd_w1, L0_cond_bwd_b1, L0_cond_bwd_w2, L0_cond_bwd_b2, L0_cond_ffada_w, L0_cond_ffada_b, L0_cond_ff_w1, L0_cond_ff_b1, L0_cond_ff_w2, L0_cond_ff_b2):
    import jax
    import jax.numpy as jnp

    def _L0_cond_ref(x, t, mask, ada_w, ada_b, ssm_w1, ssm_b1, ssm_w2, ssm_b2, bwd_w1, bwd_b1, bwd_w2, bwd_b2, ffada_w, ffada_b, ff_w1, ff_b1, ff_w2, ff_b2):
        import jax, jax.numpy as jnp
        import numpy as np
        B, L, D = (8, 512, 256)
        FF_MULT = 2
        EPS = 1e-06

        def _layernorm(x):
            mu = jnp.mean(x, axis=-1, keepdims=True)
            var = jnp.mean(jnp.square(x - mu), axis=-1, keepdims=True)
            return (x - mu) / jnp.sqrt(var + EPS)

        def _ssm_fallback(u, w1, b1, w2, b2):
            h = jax.nn.gelu(u @ w1 + b1, approximate=False)
            return h @ w2 + b2
        m = mask[:, :, None]
        emb = jax.nn.silu(t) @ ada_w + ada_b
        shift, scale, gate_msa = jnp.split(emb, 3, axis=1)
        norm = _layernorm(x) * (1.0 + scale[:, None]) + shift[:, None]
        norm = jnp.where(m, norm, 0.0)
        fwd = _ssm_fallback(norm, ssm_w1, ssm_b1, ssm_w2, ssm_b2)
        bwd = jnp.flip(_ssm_fallback(jnp.flip(norm, axis=1), bwd_w1, bwd_b1, bwd_w2, bwd_b2), axis=1)
        ssm_out = jnp.where(m, fwd + bwd, 0.0)
        x = x + gate_msa[:, None] * ssm_out
        ff_ada = jax.nn.silu(t) @ ffada_w + ffada_b
        shift_mlp, scale_mlp, gate_mlp = jnp.split(ff_ada, 3, axis=1)
        ff_norm = _layernorm(x) * (1.0 + scale_mlp[:, None]) + shift_mlp[:, None]
        h = jax.nn.gelu(ff_norm @ ff_w1 + ff_b1, approximate=True)
        ff_out = h @ ff_w2 + ff_b2
        return x + gate_mlp[:, None] * ff_out
    x = _L0_cond_ref(x, cond_1024, mask_BxS_bk0, L0_cond_ada_w, L0_cond_ada_b, L0_cond_ssm_w1, L0_cond_ssm_b1, L0_cond_ssm_w2, L0_cond_ssm_b2, L0_cond_bwd_w1, L0_cond_bwd_b1, L0_cond_bwd_w2, L0_cond_bwd_b2, L0_cond_ffada_w, L0_cond_ffada_b, L0_cond_ff_w1, L0_cond_ff_b1, L0_cond_ff_w2, L0_cond_ff_b2)
    return x

_drawn_inputs = setup_inputs


def setup_inputs(seed=0):
    import zlib

    import numpy as np

    out = dict(_drawn_inputs(seed))
    spreads = {'L0_cond_ada_b': (0.0, 0.8),
     'L0_cond_ssm_b1': (0.0, 0.8),
     'L0_cond_ssm_b2': (0.0, 0.8),
     'L0_cond_bwd_b1': (0.0, 0.8),
     'L0_cond_bwd_b2': (0.0, 0.8),
     'L0_cond_ffada_b': (0.0, 0.608),
     'L0_cond_ff_b1': (0.0, 0.8),
     'L0_cond_ff_b2': (0.0, 0.403)}
    factors = {'L0_cond_ada_w': 5.238,
     'L0_cond_ssm_w1': 8.0,
     'L0_cond_ssm_w2': 8.0,
     'L0_cond_bwd_w1': 8.0,
     'L0_cond_bwd_w2': 8.0,
     'L0_cond_ff_w1': 3.274,
     'L0_cond_ff_w2': 3.051}
    for name, (base, spread) in spreads.items():
        noise = np.random.default_rng([zlib.crc32(name.encode()), seed]).standard_normal(out[name].shape)
        drawn = base * np.exp(spread * noise) if base else spread * noise
        out[name] = jnp.asarray(drawn.astype(out[name].dtype))
    for name, factor in factors.items():
        out[name] = (out[name] * factor).astype(out[name].dtype)
    return out
```

```python
from contextlib import ExitStack

import concourse.bass as bass
from concourse import mybir

ALU = mybir.AluOpType
ACT = mybir.ActivationFunctionType
F32 = mybir.dt.float32
F32R = mybir.dt.float32r
U8 = mybir.dt.uint8

P = 128
D = 256
KD = D // P
H = 512
HC = H // P
NT = 4
BT = NT * P
BW = NT * D
EPS = 1e-6


def build(nc, x, condT, mask, ada_w, ada_b, ssm_w1, ssm_w2, bwd_w1, bwd_w2, b1, b2, ffada_w, ffada_b,
          ff_w1, ff_w2, out):
    TILES = x.shape[1] // D
    NB = TILES // NT
    ALL = 2 * NB
    PAIRS = (NB - 2) // 2
    B = condT.shape[1]

    with ExitStack() as ctx:
        def sb(name, shape, dt=F32):
            return ctx.enter_context(nc.sbuf_tensor(name, shape, dt))

        def sem(name):
            return ctx.enter_context(nc.semaphore(name))

        X = sb("X", [P, TILES * D])
        norm = sb("norm", [P, BW])
        n_hi = [sb(f"n_hi{q}", [P, KD, BT], F32R) for q in range(2)]
        n_lo = [sb(f"n_lo{q}", [P, KD, BT], F32R) for q in range(2)]
        g_hi = [sb(f"g_hi{q}", [P, HC, BT], F32R) for q in range(2)]
        g_lo = [sb(f"g_lo{q}", [P, HC, BT], F32R) for q in range(2)]
        gated = sb("gated", [P, BW])
        w1 = [sb(f"w1_{f}", [P, KD, H]) for f in range(2)]
        w1_hi = [sb(f"w1_hi{f}", [P, KD, H], F32R) for f in range(2)]
        w1_lo = [sb(f"w1_lo{f}", [P, KD, H], F32R) for f in range(2)]
        w2 = [sb(f"w2_{f}", [P, HC, D]) for f in range(2)]
        w2_hi = [sb(f"w2_hi{f}", [P, HC, D], F32R) for f in range(2)]
        w2_lo = [sb(f"w2_lo{f}", [P, HC, D], F32R) for f in range(2)]
        adaw = [sb(f"adaw{f}", [P, KD, 3 * D]) for f in range(2)]
        adab = sb("adab", [1, 2, 3 * D])
        b2s = sb("b2s", [1, 3, D])
        b1s = sb("b1s", [P, 2 * HC])
        ct = sb("ct", [P, KD, B])
        th = sb("th", [P, KD, B])
        silu = sb("silu", [P, KD, P])
        ones = sb("ones", [1, P])
        ident = sb("ident", [P, P])
        shift = [sb(f"shift{f}", [P, D]) for f in range(2)]
        scale1 = [sb(f"scale1_{f}", [P, D]) for f in range(2)]
        gate = [sb(f"gate{f}", [P, D]) for f in range(2)]
        gateb = [sb(f"gateb{f}", [P, D]) for f in range(2)]
        mask8 = sb("mask8", [P, TILES], U8)
        maskf = sb("maskf", [P, TILES])
        stats = sb("stats", [P, NT, 6])
        mv = [sb(f"mv{q}", [P, NT, 2]) for q in range(2)]
        vare = sb("vare", [P, NT])
        mhalf = sb("mhalf", [P, NT])
        rstd = [sb(f"rstd{q}", [P, NT]) for q in range(2)]

        ps_n = ctx.enter_context(nc.psum_tensor("ps_n", [P, KD, BT], F32))
        ps_h = ctx.enter_context(nc.psum_tensor("ps_h", [P, HC, BT], F32))
        ps_o = ctx.enter_context(nc.psum_tensor("ps_o", [P, NT, D], F32))

        s_cond = sem("cond_loaded")
        s_ada = [sem(f"ada_loaded{f}") for f in range(2)]
        s_bias = sem("biases_loaded")
        s_maskl = sem("mask_loaded")
        s_w1l = [sem(f"w1_loaded{f}") for f in range(2)]
        s_w2l = [sem(f"w2_loaded{f}") for f in range(2)]
        s_x = [sem(f"x_loaded{q}") for q in range(2)]
        s_const = sem("ones_set")
        s_id0 = sem("ident_zeroed")
        s_id = sem("ident_ready")
        s_tanh = sem("tanh_ready")
        s_th1 = sem("tanh_plus_one")
        s_silu = sem("silu_ready")
        s_emb = sem("emb_ready")
        s_rows = sem("shift_scale_ready")
        s_gate = sem("gate_ready")
        s_gateb = sem("gateb_ready")
        s_mask = sem("maskf_ready")
        s_wsplit_hi = sem("weights_hi_ready")
        s_wsplit = sem("weights_split")
        s_var = sem("variance_ready")
        s_stat = sem("stats_ready")
        s_aggr = sem("mean_variance_ready")
        s_rstd = sem("rstd_ready")
        s_cent = sem("centred_ready")
        s_norm = sem("norm_ready")
        s_T = sem("transposed")
        s_nhi = sem("n_hi_ready")
        s_nlo = sem("n_lo_ready")
        s_h = sem("hidden_ready")
        s_gelu = sem("gelu_ready")
        s_ghi = sem("g_hi_ready")
        s_glo = sem("g_lo_ready")
        s_o = sem("output_ready")
        s_gated = sem("gated_ready")
        s_upd = sem("update_ready")
        s_res = sem("block_done")
        s_out = [sem(f"y_stored{q}") for q in range(2)]

        block = ctx.enter_context(nc.Block())

        def blk(b):
            return X[:, bass.ds(b * BW, BW)]

        @block.sync
        def _(sp):
            sp.dma_start(ct[:], condT.rearrange("(k p) b -> p k b", p=P)).then_inc(s_cond, 16)
            sp.dma_start(adaw[0][:], ada_w.rearrange("(k p) n -> p k n", p=P)).then_inc(s_ada[0], 16)
            sp.dma_start(X[:, 0:BW], x[:, 0:BW]).then_inc(s_x[0], 16)
            for h, w in enumerate((ssm_w1, bwd_w1)):
                sp.dma_start(w1[0][:, :, h * D:(h + 1) * D],
                             w.rearrange("(k p) n -> p k n", p=P)).then_inc(s_w1l[0], 16)
            sp.dma_start(X[:, BW:2 * BW], x[:, BW:2 * BW]).then_inc(s_x[1], 16)
            for h, w in enumerate((ssm_w2, bwd_w2)):
                sp.dma_start(w2[0][:, 2 * h:2 * h + 2, :],
                             w.rearrange("(k p) n -> p k n", p=P)).then_inc(s_w2l[0], 16)
            sp.dma_start(adaw[1][:], ffada_w.rearrange("(k p) n -> p k n", p=P)).then_inc(s_ada[1], 16)
            with sp.Fori(1, NB // 2) as k:
                for q in range(2):
                    sp.wait_ge(s_x[q], 16 * k)
                    sp.dma_start(X[:, bass.ds((2 * k + q) * BW, BW)],
                                 x[:, bass.ds((2 * k + q) * BW, BW)]).then_inc(s_x[q], 16)
            sp.dma_start(w1[1][:], ff_w1.rearrange("(k p) n -> p k n", p=P)).then_inc(s_w1l[1], 16)
            sp.dma_start(w2[1][:], ff_w2.rearrange("(k p) n -> p k n", p=P)).then_inc(s_w2l[1], 16)
            with sp.Fori(0, NB // 2) as k:
                for q in range(2):
                    sp.wait_ge(s_res, 2 * k + (NB + q + 1))
                    sp.dma_start(out[:, bass.ds((2 * k + q) * BW, BW)],
                                 X[:, bass.ds((2 * k + q) * BW, BW)]).then_inc(s_out[q], 16)
            for q in range(2):
                sp.wait_ge(s_out[q], 16 * (NB // 2))

        @block.gpsimd
        def _(pool):
            nc.gpsimd.memset(ones[:], 1.0).then_inc(s_const, 1)
            nc.gpsimd.memset(mhalf[:], -0.5).then_inc(s_const, 1)
            nc.gpsimd.memset(ident[:], 0.0).then_inc(s_id0, 1)
            pool.wait_ge(s_id0, 1)
            nc.gpsimd.affine_select(out=ident[:], in_=ident[:], compare_op=ALU.not_equal, fill=1.0, base=0,
                                    pattern=[[-1, P]], channel_multiplier=1).then_inc(s_id, 1)

            def reciprocal_std(b, q):
                pool.wait_ge(s_var, b + 1)
                nc.gpsimd.tensor_tensor(rstd[q][:], vare[:], mhalf[:], ALU.pow).then_inc(s_rstd, 1)

            def add_bias(b, f):
                for j in range(2):
                    half = gated[:, 2 * j * D:(2 * j + 2) * D].rearrange("p (t d) -> p t d", d=D)
                    pool.wait_ge(s_gated, 2 * b + (j + 1))
                    nc.gpsimd.tensor_tensor(half, half, gateb[f][:].unsqueeze(1).broadcast_to([P, 2, D]),
                                            ALU.add).then_inc(s_upd, 1)

            pool.wait_ge(s_const, 2)
            reciprocal_std(0, 0)
            pool.wait_ge(s_w1l[0], 32)
            pool.wait_ge(s_wsplit_hi, 1)
            nc.gpsimd.tensor_tensor(w1_lo[0][:], w1[0][:], w1_hi[0][:].bitcast(F32),
                                    ALU.subtract).then_inc(s_wsplit, 1)
            reciprocal_std(1, 1)
            pool.wait_ge(s_wsplit_hi, 2)
            nc.gpsimd.tensor_tensor(w2_lo[0][:], w2[0][:], w2_hi[0][:].bitcast(F32),
                                    ALU.subtract).then_inc(s_wsplit, 1)
            pool.wait_ge(s_gateb, 1)

            def step(i, q, fprev):
                reciprocal_std(i + 2, q)
                add_bias(i - 1, fprev)

            reciprocal_std(2, 0)
            with pool.Fori(0, PAIRS) as k:
                step(2 * k + 1, 1, 0)
                step(2 * k + 2, 0, 0)
            for n, (src, hi, lo, loaded) in enumerate(((w1[1], w1_hi[1], w1_lo[1], s_w1l[1]),
                                                       (w2[1], w2_hi[1], w2_lo[1], s_w2l[1]))):
                pool.wait_ge(loaded, 16)
                nc.gpsimd.tensor_copy(hi[:], src[:]).then_inc(s_wsplit_hi, 1)
                pool.wait_ge(s_wsplit_hi, 3 + n)
                nc.gpsimd.tensor_tensor(lo[:], src[:], hi[:].bitcast(F32), ALU.subtract).then_inc(s_wsplit, 1)
            step(NB - 1, 1, 0)
            step(NB, 0, 0)
            pool.wait_ge(s_gateb, 2)
            with pool.Fori(0, PAIRS - 1) as k:
                step(2 * k + (NB + 1), 1, 1)
                step(2 * k + (NB + 2), 0, 1)
            step(ALL - 3, 1, 1)
            for b in range(ALL - 3, ALL):
                add_bias(b, 1)

        @block.scalar
        def _(act):
            act.dma_start(adab[0:1, 0, :], ada_b).then_inc(s_bias, 16)
            act.dma_start(adab[0:1, 1, :], ffada_b).then_inc(s_bias, 16)
            act.dma_start(b2s[:], b2).then_inc(s_bias, 16)
            act.dma_start(b1s[:], b1).then_inc(s_bias, 16)
            act.dma_start(mask8[:], mask).then_inc(s_maskl, 16)
            act.wait_ge(s_cond, 16)
            nc.scalar.activation(th[:], ct[:], ACT.Tanh, scale=0.5).then_inc(s_tanh, 1)
            act.wait_ge(s_w1l[0], 32)
            nc.scalar.activation(w1_hi[0][:], w1[0][:], ACT.Copy).then_inc(s_wsplit_hi, 1)

            def n_high(b, q):
                act.wait_ge(s_T, b + 1)
                for k in range(KD):
                    nc.scalar.activation(n_hi[q][:, k, :], ps_n[:, k, :], ACT.Copy).then_inc(s_nhi, 1)

            def gelu(i, q, f, c):
                func = (ACT.Gelu, ACT.Gelu_apprx_tanh)[f]
                act.wait_ge(s_h, HC * i + (c + 1))
                nc.scalar.activation(ps_h[:, c, :], ps_h[:, c, :], func,
                                     bias=b1s[:, f * HC + c:f * HC + c + 1]).then_inc(s_gelu, 1)
                act.wait_ge(s_gelu, HC * i + (c + 1))
                nc.scalar.activation(g_hi[q][:, c, :], ps_h[:, c, :], ACT.Copy).then_inc(s_ghi, 1)

            def step(i, q, f, last=False):
                gelu(i, q, f, 0)
                gelu(i, q, f, 1)
                if not last:
                    n_high(i + 1, 1 - q)
                gelu(i, q, f, 2)
                gelu(i, q, f, 3)

            n_high(0, 0)
            act.wait_ge(s_w2l[0], 32)
            nc.scalar.activation(w2_hi[0][:], w2[0][:], ACT.Copy).then_inc(s_wsplit_hi, 1)
            act.wait_ge(s_bias, 64)
            step(0, 0, 0)
            with act.Fori(0, PAIRS) as k:
                step(2 * k + 1, 1, 0)
                step(2 * k + 2, 0, 0)
            step(NB - 1, 1, 0)
            step(NB, 0, 1)
            with act.Fori(0, PAIRS) as k:
                step(2 * k + (NB + 1), 1, 1)
                step(2 * k + (NB + 2), 0, 1)
            step(ALL - 1, 1, 1, last=True)

        @block.vector
        def _(dve):
            def tile_stats(b, f, q, first=False):
                tok = b - NB * f
                if f == 0:
                    dve.wait_ge(s_x[q], 16 if first else 8 * b + (16 - 8 * q))
                else:
                    dve.wait_ge(s_res, b - (NB - 1))
                for t in range(NT):
                    ins = nc.vector.bn_stats(stats[:, t, :], X[:, bass.ds(tok * BW + t * D, D)])
                ins.then_inc(s_stat, 1)

            def variance(b, q):
                for t in range(NT):
                    ins = nc.vector.bn_aggr(mv[q][:, t, :], stats[:, t, :])
                ins.then_inc(s_aggr, 1)
                dve.wait_ge(s_aggr, b + 1)
                nc.vector.tensor_scalar(vare[:], mv[q][:, :, 1], EPS, None, ALU.add).then_inc(s_var, 1)

            def modulate(b, q, f, first=False):
                tok = b - NB * f
                if not first:
                    dve.wait_ge(s_T, b)
                for t in range(NT):
                    ins = nc.vector.scalar_tensor_tensor(
                        norm[:, t * D:(t + 1) * D], X[:, bass.ds(tok * BW + t * D, D)], mv[q][:, t, 0:1],
                        scale1[f][:], ALU.subtract, ALU.mult)
                ins.then_inc(s_cent, 1)
                dve.wait_ge(s_cent, b + 1)
                dve.wait_ge(s_rstd, b + 1)
                for t in range(NT):
                    ins = nc.vector.scalar_tensor_tensor(
                        norm[:, t * D:(t + 1) * D], norm[:, t * D:(t + 1) * D], rstd[q][:, t:t + 1],
                        shift[f][:], ALU.mult, ALU.add)
                ins.then_inc(s_norm, 1)

            def n_low(b, q):
                for k in range(KD):
                    dve.wait_ge(s_nhi, KD * b + (k + 1))
                    nc.vector.tensor_tensor(n_lo[q][:, k, :], ps_n[:, k, :], n_hi[q][:, k, :].bitcast(F32),
                                            ALU.subtract).then_inc(s_nlo, 1)

            def g_low(i, q, c):
                dve.wait_ge(s_ghi, HC * i + (c + 1))
                nc.vector.tensor_tensor(g_lo[q][:, c, :], ps_h[:, c, :], g_hi[q][:, c, :].bitcast(F32),
                                        ALU.subtract).then_inc(s_glo, 1)

            def gate_half(b, f, j, first=False):
                if j == 0 and not first:
                    dve.wait_ge(s_res, b)
                dve.wait_ge(s_o, 2 * b + (j + 1))
                nc.vector.tensor_tensor(
                    gated[:, 2 * j * D:(2 * j + 2) * D].rearrange("p (t d) -> p t d", d=D),
                    ps_o[:, 2 * j:2 * j + 2, :], gate[f][:].unsqueeze(1).broadcast_to([P, 2, D]),
                    ALU.mult).then_inc(s_gated, 1)

            def residual(b, f):
                tok = b - NB * f
                dve.wait_ge(s_upd, 2 * b + 2)
                if f == 0:
                    for t in range(NT):
                        xt = X[:, bass.ds(tok * BW + t * D, D)]
                        ins = nc.vector.scalar_tensor_tensor(xt, gated[:, t * D:(t + 1) * D],
                                                             maskf[:, bass.ds(tok * NT + t, 1)], xt,
                                                             ALU.mult, ALU.add)
                    ins.then_inc(s_res, 1)
                else:
                    nc.vector.tensor_tensor(blk(tok), gated[:], blk(tok), ALU.add).then_inc(s_res, 1)

            def shift_scale_rows(f):
                dve.wait_ge(s_emb, f + 1)
                nc.vector.tensor_scalar(scale1[f][:], ps_h[:, 2 * f, D:2 * D], 1.0, None,
                                        ALU.add).then_inc(s_rows, 1)
                nc.vector.tensor_copy(shift[f][:], ps_h[:, 2 * f, 0:D]).then_inc(s_rows, 1)

            def gate_rows(f):
                nc.vector.tensor_copy(gate[f][:], ps_h[:, 2 * f + 1, 0:D]).then_inc(s_gate, 1)
                dve.wait_ge(s_gate, f + 1)
                nc.vector.tensor_tensor(gateb[f][:], ps_h[:, 2 * f + 1, D:2 * D], gate[f][:],
                                        ALU.mult).then_inc(s_gateb, 1)

            def step(i, q, fprev, fnext, first=False, second=False, last=False, tail=False):
                g_low(i, q, 0)
                if not first and not second:
                    residual(i - 2, fprev[0])
                if not tail:
                    tile_stats(i + 2, fnext, q)
                    dve.wait_ge(s_stat, i + 3)
                g_low(i, q, 1)
                if not tail:
                    variance(i + 2, q)
                if not last:
                    n_low(i + 1, 1 - q)
                if not first:
                    gate_half(i - 1, fprev[1], 0, first=second)
                if not tail:
                    modulate(i + 2, q, fnext)
                g_low(i, q, 2)
                g_low(i, q, 3)
                if not first:
                    gate_half(i - 1, fprev[1], 1)

            def first_variance(b, q):
                tile_stats(b, 0, q, first=True)
                dve.wait_ge(s_stat, b + 1)
                variance(b, q)

            first_variance(0, 0)
            dve.wait_ge(s_tanh, 1)
            nc.vector.tensor_scalar(th[:], th[:], 1.0, 0.5, ALU.add, ALU.mult).then_inc(s_th1, 1)
            dve.wait_ge(s_th1, 1)
            nc.vector.tensor_tensor(silu[:].rearrange("p k (b r) -> p (k b) r", r=P // B),
                                    th[:].rearrange("p k b -> p (k b)").unsqueeze(2).broadcast_to([P, KD * B, P // B]),
                                    ct[:].rearrange("p k b -> p (k b)").unsqueeze(2).broadcast_to([P, KD * B, P // B]),
                                    ALU.mult).then_inc(s_silu, 1)
            shift_scale_rows(0)
            dve.wait_ge(s_rows, 2)
            modulate(0, 0, 0, first=True)
            dve.wait_ge(s_rstd, 1)
            first_variance(1, 1)
            dve.wait_ge(s_maskl, 16)
            nc.vector.tensor_copy(maskf[:], mask8[:]).then_inc(s_mask, 1)
            gate_rows(0)
            n_low(0, 0)
            modulate(1, 1, 0)
            shift_scale_rows(1)
            gate_rows(1)
            dve.wait_ge(s_rows, 4)
            dve.wait_ge(s_mask, 1)
            step(0, 0, (0, 0), 0, first=True)
            step(1, 1, (0, 0), 0, second=True)
            step(2, 0, (0, 0), 0)
            with dve.Fori(1, PAIRS - 1) as k:
                step(2 * k + 1, 1, (0, 0), 0)
                step(2 * k + 2, 0, (0, 0), 0)
            step(NB - 3, 1, (0, 0), 0)
            step(NB - 2, 0, (0, 0), 1)
            step(NB - 1, 1, (0, 0), 1)
            step(NB, 0, (0, 0), 1)
            step(NB + 1, 1, (0, 1), 1)
            step(NB + 2, 0, (1, 1), 1)
            with dve.Fori(1, PAIRS - 1) as k:
                step(2 * k + (NB + 1), 1, (1, 1), 1)
                step(2 * k + (NB + 2), 0, (1, 1), 1)
            step(ALL - 3, 1, (1, 1), 1)
            step(ALL - 2, 0, (1, 1), 1, tail=True)
            step(ALL - 1, 1, (1, 1), 1, tail=True, last=True)
            residual(ALL - 2, 1)
            gate_half(ALL - 1, 1, 0)
            gate_half(ALL - 1, 1, 1)
            residual(ALL - 1, 1)

        @block.tensor
        def _(pe):
            def embed(f):
                pe.wait_ge(s_ada[f], 16)
                for lo, hi, dst in ((0, 2 * D, ps_h[:, 2 * f, :]), (2 * D, 3 * D, ps_h[:, 2 * f + 1, 0:D])):
                    for k in range(KD):
                        nc.tensor.matmul(dst, silu[:, k, :], adaw[f][:, k, lo:hi], start=(k == 0), stop=False)
                    nc.tensor.matmul(dst, ones[:], adab[0:1, f, lo:hi], start=False, stop=True)
                rows = ((0, 1), (2,))[f]
                for r in rows:
                    last = nc.tensor.matmul(ps_h[:, 2 * f + 1, D:2 * D], ones[:], b2s[0:1, r, :],
                                            start=(r == rows[0]), stop=(r == rows[-1]))
                last.then_inc(s_emb, 1)

            def transposes(b, first=False):
                pe.wait_ge(s_norm, b + 1)
                if not first:
                    pe.wait_ge(s_nlo, KD * b)
                for t in range(NT):
                    for k in range(KD):
                        last = nc.tensor.transpose(ps_n[:, k, t * P:(t + 1) * P],
                                                   norm[:, t * D + k * P:t * D + (k + 1) * P], ident[:])
                last.then_inc(s_T, 1)

            def first_product(i, q, f, c, first=False):
                if c == 0:
                    pe.wait_ge(s_nlo, KD * i + KD)
                if not first:
                    pe.wait_ge(s_glo, HC * i + (c + 1 - HC))
                for k in range(KD):
                    for w, n in ((w1_hi[f], n_hi[q]), (w1_hi[f], n_lo[q]), (w1_lo[f], n_hi[q])):
                        last = nc.tensor.matmul(ps_h[:, c, :], w[:, k, c * P:(c + 1) * P], n[:, k, :],
                                                start=(k == 0 and w is w1_hi[f] and n is n_hi[q]),
                                                stop=(k == KD - 1 and w is w1_lo[f]))
                last.then_inc(s_h, 1)

            def second_product(b, q, f, t, first=False):
                if t == 0:
                    pe.wait_ge(s_glo, HC * b + HC)
                if t % 2 == 0 and not first:
                    pe.wait_ge(s_gated, 2 * b + (t // 2 - 1))
                for c in range(HC):
                    for n, (g, w) in enumerate(((g_hi[q], w2_hi[f]), (g_hi[q], w2_lo[f]), (g_lo[q], w2_hi[f]))):
                        last = nc.tensor.matmul(ps_o[:, t, :], g[:, c, t * P:(t + 1) * P], w[:, c, :],
                                                start=(c == 0 and n == 0), stop=(c == HC - 1 and n == 2))
                if t % 2 == 1:
                    last.then_inc(s_o, 1)

            def step(i, q, f, fprev, first=False, second=False, last=False):
                for c in range(HC):
                    first_product(i, q, f, c, first)
                    if c == 1 and not last:
                        transposes(i + 1)
                    if not first:
                        second_product(i - 1, 1 - q, fprev, c, first=second)

            pe.wait_ge(s_const, 2)
            pe.wait_ge(s_bias, 64)
            pe.wait_ge(s_silu, 1)
            embed(0)
            pe.wait_ge(s_id, 1)
            transposes(0, first=True)
            embed(1)
            pe.wait_ge(s_gateb, 2)
            pe.wait_ge(s_wsplit, 1)
            step(0, 0, 0, 0, first=True)
            pe.wait_ge(s_wsplit, 2)
            step(1, 1, 0, 0, second=True)
            step(2, 0, 0, 0)
            with pe.Fori(1, PAIRS) as k:
                step(2 * k + 1, 1, 0, 0)
                step(2 * k + 2, 0, 0, 0)
            step(NB - 1, 1, 0, 0)
            pe.wait_ge(s_wsplit, 4)
            step(NB, 0, 1, 0)
            with pe.Fori(0, PAIRS) as k:
                step(2 * k + (NB + 1), 1, 1, 1)
                step(2 * k + (NB + 2), 0, 1, 1)
            step(ALL - 1, 1, 1, 1, last=True)
            for t in range(NT):
                second_product(ALL - 1, 1, 1, t)


def kernel(**inputs):
    import numpy as np
    import concourse.bacc as bacc
    from concourse import mybir as my
    from concourse.bass_utils import run_bass_kernel_spmd

    a = {k: np.asarray(v) for k, v in inputs.items()}
    L = "L0_cond_"
    cols = lambda v: v.reshape(-1, 128).T
    arrays = {
        "x": a["x"].reshape(128, -1),
        "condT": a["cond_1024"].T,
        "mask": a["mask_BxS_bk0"].reshape(128, -1),
        "ada_w": a[L + "ada_w"], "ada_b": a[L + "ada_b"].reshape(1, -1),
        "ssm_w1": a[L + "ssm_w1"], "ssm_w2": a[L + "ssm_w2"],
        "bwd_w1": a[L + "bwd_w1"], "bwd_w2": a[L + "bwd_w2"],
        "b1": np.concatenate([cols(a[L + n]) for n in ("ssm_b1", "bwd_b1", "ff_b1")], axis=1),
        "b2": np.stack([a[L + n] for n in ("ssm_b2", "bwd_b2", "ff_b2")])[None],
        "ffada_w": a[L + "ffada_w"], "ffada_b": a[L + "ffada_b"].reshape(1, -1),
        "ff_w1": a[L + "ff_w1"], "ff_w2": a[L + "ff_w2"],
    }
    arrays = {k: np.ascontiguousarray(v) for k, v in arrays.items()}
    nc = bacc.Bacc("TRN2", target_bir_lowering=False, num_devices=1)
    args = [nc.dram_tensor(k, v.shape, my.dt.from_np(v.dtype), kind="ExternalInput").ap()
            for k, v in arrays.items()]
    out = nc.dram_tensor("y", arrays["x"].shape, my.dt.float32, kind="ExternalOutput").ap()
    build(nc, *args, out)
    r = run_bass_kernel_spmd(nc, [arrays], core_ids=[0])
    return r.results[0]["y"].reshape(a["x"].shape)
```

```python
from contextlib import ExitStack

import concourse.bass as bass
from concourse import mybir

ALU = mybir.AluOpType
ACT = mybir.ActivationFunctionType
F32 = mybir.dt.float32
F32R = mybir.dt.float32r
U8 = mybir.dt.uint8

P = 128
D = 256
KD = D // P
H = 512
HC = H // P
NT = 4
BT = NT * P
BW = NT * D
EPS = 1e-6
WARM = (12, 14, 5)


def build(nc, x, condT, mask, ada_w, ada_b, ssm_w1, ssm_w2, bwd_w1, bwd_w2, b1, b2, ffada_w, ffada_b,
          ff_w1, ff_w2, out):
    TILES = x.shape[1] // D
    NB = TILES // NT
    ALL = 2 * NB
    PAIRS = (NB - 2) // 2
    B = condT.shape[1]

    with ExitStack() as ctx:
        def sb(name, shape, dt=F32):
            return ctx.enter_context(nc.sbuf_tensor(name, shape, dt))

        def sem(name):
            return ctx.enter_context(nc.semaphore(name))

        X = sb("X", [P, TILES * D])
        xhat = sb("xhat", [P, BW])
        norm = sb("norm", [P, BW])
        n_hi = [sb(f"n_hi{q}", [P, KD, BT], F32R) for q in range(2)]
        n_lo = [sb(f"n_lo{q}", [P, KD, BT], F32R) for q in range(2)]
        g_hi = [sb(f"g_hi{q}", [P, HC, BT], F32R) for q in range(2)]
        g_lo = [sb(f"g_lo{q}", [P, HC, BT], F32R) for q in range(2)]
        gated = sb("gated", [P, BW])
        w1 = [sb(f"w1_{f}", [P, KD, H]) for f in range(2)]
        w1_hi = [sb(f"w1_hi{f}", [P, KD, H], F32R) for f in range(2)]
        w1_lo = [sb(f"w1_lo{f}", [P, KD, H], F32R) for f in range(2)]
        w2 = [sb(f"w2_{f}", [P, HC, D]) for f in range(2)]
        w2_hi = [sb(f"w2_hi{f}", [P, HC, D], F32R) for f in range(2)]
        w2_lo = [sb(f"w2_lo{f}", [P, HC, D], F32R) for f in range(2)]
        adaw = [sb(f"adaw{f}", [P, KD, 3 * D]) for f in range(2)]
        adab = sb("adab", [P, 2, 3 * D])
        b2s = sb("b2s", [P, 3, D])
        b1s = sb("b1s", [P, 2 * HC])
        ct = sb("ct", [P, KD, B])
        th = sb("th", [P, KD, B])
        silu = sb("silu", [P, KD, P])
        warm = sb("warm", [P, BT], mybir.dt.bfloat16)
        ident = sb("ident", [P, P])
        shift = [sb(f"shift{f}", [P, D]) for f in range(2)]
        scale1 = [sb(f"scale1_{f}", [P, D]) for f in range(2)]
        gate = [sb(f"gate{f}", [P, D]) for f in range(2)]
        gateb = [sb(f"gateb{f}", [P, D]) for f in range(2)]
        mask8 = sb("mask8", [P, TILES], U8)
        maskf = sb("maskf", [P, TILES])
        stats = sb("stats", [P, NT, 6])
        mv = [sb(f"mv{q}", [P, NT, 2]) for q in range(2)]
        nmr = [sb(f"nmr{q}", [P, NT]) for q in range(2)]
        vare = sb("vare", [P, NT])
        mhalf = sb("mhalf", [P, NT])
        rstd = [sb(f"rstd{q}", [P, NT]) for q in range(2)]

        ps_n = ctx.enter_context(nc.psum_tensor("ps_n", [P, KD, BT], F32))
        ps_h = ctx.enter_context(nc.psum_tensor("ps_h", [P, HC, BT], F32))
        ps_o = ctx.enter_context(nc.psum_tensor("ps_o", [P, NT, D], F32))

        s_cond = sem("cond_loaded")
        s_ada = [sem(f"ada_loaded{f}") for f in range(2)]
        s_adag = [sem(f"ada_gate_loaded{f}") for f in range(2)]
        s_bias = sem("b1_loaded")
        s_adab = [sem(f"ada_b_loaded{f}") for f in range(2)]
        s_b2 = sem("b2_loaded")
        s_maskl = sem("mask_loaded")
        s_w1l = [sem(f"w1_loaded{f}") for f in range(2)]
        s_w2l = [sem(f"w2_loaded{f}") for f in range(2)]
        s_x = [sem(f"x_loaded{q}") for q in range(2)]
        s_const = sem("exponent_set")
        s_warm = sem("warm_set")
        s_id0 = sem("ident_zeroed")
        s_id = sem("ident_ready")
        s_tanh = sem("tanh_ready")
        s_th1 = sem("tanh_plus_one")
        s_silu = sem("silu_ready")
        s_emb = sem("emb_ready")
        s_rows = sem("shift_scale_ready")
        s_gate = sem("gate_ready")
        s_gateb = sem("gateb_ready")
        s_mask = sem("maskf_ready")
        s_wsplit_hi = sem("weights_hi_ready")
        s_wsplit = sem("weights_split")
        s_var = sem("variance_ready")
        s_stat = sem("stats_ready")
        s_aggr = sem("mean_variance_ready")
        s_rstd = sem("rstd_ready")
        s_nmr = sem("nmr_ready")
        s_xhat = sem("xhat_ready")
        s_scaled = sem("scaled_ready")
        s_norm = sem("norm_ready")
        s_norm0 = sem("norm0_step")
        s_half0 = sem("norm0_half_ready")
        s_T = sem("transposed")
        s_nhi = sem("n_hi_ready")
        s_nlo = sem("n_lo_ready")
        s_h = sem("hidden_ready")
        s_gelu = sem("gelu_ready")
        s_ghi = sem("g_hi_ready")
        s_glo = sem("g_lo_ready")
        s_o = sem("output_ready")
        s_gated = sem("gated_ready")
        s_upd = sem("update_ready")
        s_res = sem("block_done")
        s_pre = sem("last_bias_added")
        s_tail = sem("last_half_done")
        s_out = [sem(f"y_stored{q}") for q in range(2)]
        s_outh = [sem(f"last_half_stored{j}") for j in range(2)]

        block = ctx.enter_context(nc.Block())

        def blk(b):
            return X[:, bass.ds(b * BW, BW)]

        @block.sync
        def _(sp):
            def store(b, q):
                sp.wait_ge(s_res, b + (NB + 1))
                sp.dma_start(out[:, bass.ds(b * BW, BW)],
                             X[:, bass.ds(b * BW, BW)]).then_inc(s_out[q], 16)

            def load_x(b, q):
                sp.dma_start(X[:, bass.ds(b * BW, BW)], x[:, bass.ds(b * BW, BW)]).then_inc(s_x[q], 16)

            def load_ada(f, lo, hi, w, loaded):
                sp.dma_start(adaw[f][:, :, lo:hi],
                             w[:, lo:hi].rearrange("(k p) n -> p k n", p=P)).then_inc(loaded, 16)

            sp.dma_start(ct[:], condT.rearrange("(k p) b -> p k b", p=P)).then_inc(s_cond, 16)
            load_x(0, 0)
            load_x(1, 1)
            load_ada(0, 0, 2 * D, ada_w, s_ada[0])
            sp.dma_start(adab[:, 0, :], ada_b.broadcast_to([P, 3 * D])).then_inc(s_adab[0], 16)
            for h, w in enumerate((ssm_w1, bwd_w1)):
                sp.dma_start(w1[0][:, :, h * D:(h + 1) * D],
                             w.rearrange("(k p) n -> p k n", p=P)).then_inc(s_w1l[0], 16)
            sp.wait_ge(s_x[0], 16)
            load_x(2, 0)
            for h, w in enumerate((ssm_w2, bwd_w2)):
                sp.dma_start(w2[0][:, 2 * h:2 * h + 2, :],
                             w.rearrange("(k p) n -> p k n", p=P)).then_inc(s_w2l[0], 16)
            load_ada(1, 0, 2 * D, ffada_w, s_ada[1])
            load_ada(0, 2 * D, 3 * D, ada_w, s_adag[0])
            load_ada(1, 2 * D, 3 * D, ffada_w, s_adag[1])
            sp.dma_start(adab[:, 1, :], ffada_b.broadcast_to([P, 3 * D])).then_inc(s_adab[1], 16)
            sp.dma_start(b2s[:], b2.broadcast_to([P, 3, D])).then_inc(s_b2, 16)
            sp.wait_ge(s_x[1], 16)
            load_x(3, 1)
            with sp.Fori(2, NB // 2) as k:
                for q in range(2):
                    sp.wait_ge(s_x[q], 16 * k)
                    load_x(2 * k + q, q)
            sp.dma_start(w1[1][:], ff_w1.rearrange("(k p) n -> p k n", p=P)).then_inc(s_w1l[1], 16)
            sp.dma_start(w2[1][:], ff_w2.rearrange("(k p) n -> p k n", p=P)).then_inc(s_w2l[1], 16)
            with sp.Fori(0, NB // 2 - 1) as k:
                for q in range(2):
                    store(2 * k + q, q)
            store(NB - 2, 0)
            for j in range(2):
                half = slice((NB - 1) * BW + 2 * j * D, (NB - 1) * BW + (2 * j + 2) * D)
                sp.wait_ge(s_tail, j + 1)
                sp.dma_start(out[:, half], X[:, half]).then_inc(s_outh[j], 16)
            sp.wait_ge(s_out[0], 16 * (NB // 2))
            sp.wait_ge(s_out[1], 16 * (NB // 2 - 1))
            for j in range(2):
                sp.wait_ge(s_outh[j], 16)

        @block.gpsimd
        def _(pool):
            nc.gpsimd.memset(warm[:], 0.0).then_inc(s_warm, 1)
            nc.gpsimd.memset(mhalf[:], -0.5).then_inc(s_const, 1)
            nc.gpsimd.memset(ident[:], 0.0).then_inc(s_id0, 1)
            pool.wait_ge(s_id0, 1)
            nc.gpsimd.affine_select(out=ident[:], in_=ident[:], compare_op=ALU.not_equal, fill=1.0, base=0,
                                    pattern=[[-1, P]], channel_multiplier=1).then_inc(s_id, 1)

            def reciprocal_std(b, q):
                pool.wait_ge(s_var, b + 1)
                nc.gpsimd.tensor_tensor(rstd[q][:], vare[:], mhalf[:], ALU.pow).then_inc(s_rstd, 1)

            def add_bias(b, f, j):
                half = gated[:, 2 * j * D:(2 * j + 2) * D].rearrange("p (t d) -> p t d", d=D)
                pool.wait_ge(s_gated, 2 * b + (j + 1))
                nc.gpsimd.tensor_tensor(half, half, gateb[f][:].unsqueeze(1).broadcast_to([P, 2, D]),
                                        ALU.add).then_inc(s_upd, 1)

            def add_shift(b, f):
                nt = norm[:].rearrange("p (t d) -> p t d", d=D)
                pool.wait_ge(s_scaled, b)
                nc.gpsimd.tensor_tensor(nt, nt, shift[f][:].unsqueeze(1).broadcast_to([P, NT, D]),
                                        ALU.add).then_inc(s_norm, 1)

            def split_lo(lo, src, hi, loaded, n):
                pool.wait_ge(loaded[0], loaded[1])
                pool.wait_ge(s_wsplit_hi, n)
                nc.gpsimd.tensor_tensor(lo[:], src[:], hi[:].bitcast(F32), ALU.subtract).then_inc(s_wsplit, 1)

            pool.wait_ge(s_const, 1)
            reciprocal_std(0, 0)
            reciprocal_std(1, 1)
            split_lo(w1_lo[0], w1[0], w1_hi[0], (s_w1l[0], 32), 1)
            add_shift(1, 0)
            split_lo(w2_lo[0], w2[0], w2_hi[0], (s_w2l[0], 32), 2)

            def step(i, q, fprev, fnext, first=False, second=False, tail=False):
                if not first and not second:
                    add_bias(i - 2, fprev[0], 1)
                if not tail:
                    reciprocal_std(i + 2, q)
                if not first:
                    add_bias(i - 1, fprev[1], 0)
                if not tail:
                    add_shift(i + 2, fnext)

            step(0, 0, (0, 0), 0, first=True)
            pool.wait_ge(s_gateb, 2)
            step(1, 1, (0, 0), 0, second=True)
            step(2, 0, (0, 0), 0)
            with pool.Fori(1, PAIRS - 1) as k:
                step(2 * k + 1, 1, (0, 0), 0)
                step(2 * k + 2, 0, (0, 0), 0)
            step(NB - 3, 1, (0, 0), 0)
            split_lo(w1_lo[1], w1[1], w1_hi[1], (s_w1l[1], 16), 3)
            step(NB - 2, 0, (0, 0), 1)
            split_lo(w2_lo[1], w2[1], w2_hi[1], (s_w2l[1], 16), 4)
            step(NB - 1, 1, (0, 0), 1)
            step(NB, 0, (0, 0), 1)
            step(NB + 1, 1, (0, 1), 1)
            step(NB + 2, 0, (1, 1), 1)
            with pool.Fori(1, PAIRS - 1) as k:
                step(2 * k + (NB + 1), 1, (1, 1), 1)
                step(2 * k + (NB + 2), 0, (1, 1), 1)
            step(ALL - 3, 1, (1, 1), 1)
            step(ALL - 2, 0, (1, 1), 1, tail=True)
            step(ALL - 1, 1, (1, 1), 1, tail=True)
            add_bias(ALL - 2, 1, 1)

        @block.scalar
        def _(act):
            act.wait_ge(s_cond, 16)
            nc.scalar.activation(th[:], ct[:], ACT.Tanh, scale=0.5).then_inc(s_tanh, 1)
            act.dma_start(b1s[:], b1).then_inc(s_bias, 16)
            act.dma_start(mask8[:], mask).then_inc(s_maskl, 16)

            def split_hi(dst, src, loaded, n):
                act.wait_ge(loaded, n)
                nc.scalar.activation(dst[:], src[:], ACT.Copy).then_inc(s_wsplit_hi, 1)

            def normalise(b, q, f, first=False):
                tok = b - NB * f
                act.wait_ge(s_nmr, b + 1)
                if not first:
                    act.wait_ge(s_scaled, b - 1)
                for t in range(NT):
                    ins = nc.scalar.activation(xhat[:, t * D:(t + 1) * D], X[:, bass.ds(tok * BW + t * D, D)],
                                               ACT.Identity, bias=nmr[q][:, t:t + 1], scale=rstd[q][:, t:t + 1])
                ins.then_inc(s_xhat, 1)

            def n_high(b, q):
                act.wait_ge(s_T, b + 1)
                for k in range(KD):
                    nc.scalar.activation(n_hi[q][:, k, :], ps_n[:, k, :], ACT.Copy).then_inc(s_nhi, 1)

            def gelu(i, q, f, c):
                func = (ACT.Gelu, ACT.Gelu_apprx_tanh)[f]
                act.wait_ge(s_h, HC * i + (c + 1))
                nc.scalar.activation(ps_h[:, c, :], ps_h[:, c, :], func,
                                     bias=b1s[:, f * HC + c:f * HC + c + 1]).then_inc(s_gelu, 1)
                act.wait_ge(s_gelu, HC * i + (c + 1))
                nc.scalar.activation(g_hi[q][:, c, :], ps_h[:, c, :], ACT.Copy).then_inc(s_ghi, 1)

            def step(i, q, f, fnext, last=False, tail=False):
                gelu(i, q, f, 0)
                gelu(i, q, f, 1)
                if not last:
                    n_high(i + 1, 1 - q)
                if not tail:
                    normalise(i + 2, q, fnext)
                gelu(i, q, f, 2)
                gelu(i, q, f, 3)

            normalise(1, 1, 0, first=True)
            split_hi(w1_hi[0], w1[0], s_w1l[0], 32)
            n_high(0, 0)
            split_hi(w2_hi[0], w2[0], s_w2l[0], 32)
            act.wait_ge(s_bias, 16)
            step(0, 0, 0, 0)
            with act.Fori(0, PAIRS - 1) as k:
                step(2 * k + 1, 1, 0, 0)
                step(2 * k + 2, 0, 0, 0)
            step(NB - 3, 1, 0, 0)
            split_hi(w1_hi[1], w1[1], s_w1l[1], 16)
            step(NB - 2, 0, 0, 1)
            split_hi(w2_hi[1], w2[1], s_w2l[1], 16)
            step(NB - 1, 1, 0, 1)
            step(NB, 0, 1, 1)
            with act.Fori(0, PAIRS - 1) as k:
                step(2 * k + (NB + 1), 1, 1, 1)
                step(2 * k + (NB + 2), 0, 1, 1)
            step(ALL - 3, 1, 1, 1)
            step(ALL - 2, 0, 1, 1, tail=True)
            step(ALL - 1, 1, 1, 1, tail=True, last=True)

        @block.vector
        def _(dve):
            def tile_stats(b, f, q, first=False):
                tok = b - NB * f
                if f == 0:
                    dve.wait_ge(s_x[q], 16 if first else 8 * b + (16 - 8 * q))
                else:
                    dve.wait_ge(s_res, b - (NB - 1))
                for t in range(NT):
                    ins = nc.vector.bn_stats(stats[:, t, :], X[:, bass.ds(tok * BW + t * D, D)])
                ins.then_inc(s_stat, 1)

            def variance(b, q):
                for t in range(NT):
                    ins = nc.vector.bn_aggr(mv[q][:, t, :], stats[:, t, :])
                ins.then_inc(s_aggr, 1)
                dve.wait_ge(s_aggr, b + 1)
                nc.vector.tensor_scalar(vare[:], mv[q][:, :, 1], EPS, None, ALU.add).then_inc(s_var, 1)

            def neg_mean_rstd(b, q):
                dve.wait_ge(s_rstd, b + 1)
                nc.vector.scalar_tensor_tensor(nmr[q][:], mv[q][:, :, 0], -1.0, rstd[q][:],
                                               ALU.mult, ALU.mult).then_inc(s_nmr, 1)

            def scale_rows(b, f):
                dve.wait_ge(s_T, b)
                dve.wait_ge(s_xhat, b)
                return nc.vector.tensor_tensor(
                    norm[:].rearrange("p (t d) -> p t d", d=D), xhat[:].rearrange("p (t d) -> p t d", d=D),
                    scale1[f][:].unsqueeze(1).broadcast_to([P, NT, D]), ALU.mult).then_inc(s_scaled, 1)

            def n_low(b, q):
                for k in range(KD):
                    dve.wait_ge(s_nhi, KD * b + (k + 1))
                    nc.vector.tensor_tensor(n_lo[q][:, k, :], ps_n[:, k, :], n_hi[q][:, k, :].bitcast(F32),
                                            ALU.subtract).then_inc(s_nlo, 1)

            def g_low(i, q, c):
                dve.wait_ge(s_ghi, HC * i + (c + 1))
                nc.vector.tensor_tensor(g_lo[q][:, c, :], ps_h[:, c, :], g_hi[q][:, c, :].bitcast(F32),
                                        ALU.subtract).then_inc(s_glo, 1)

            def gate_half(b, f, j, first=False):
                if j == 0 and not first:
                    dve.wait_ge(s_res, b)
                dve.wait_ge(s_o, 2 * b + (j + 1))
                nc.vector.tensor_tensor(
                    gated[:, 2 * j * D:(2 * j + 2) * D].rearrange("p (t d) -> p t d", d=D),
                    ps_o[:, 2 * j:2 * j + 2, :], gate[f][:].unsqueeze(1).broadcast_to([P, 2, D]),
                    ALU.mult).then_inc(s_gated, 1)

            def residual(b, f):
                tok = b - NB * f
                dve.wait_ge(s_upd, 2 * b + 2)
                if f == 0:
                    for t in range(NT):
                        xt = X[:, bass.ds(tok * BW + t * D, D)]
                        ins = nc.vector.scalar_tensor_tensor(xt, gated[:, t * D:(t + 1) * D],
                                                             maskf[:, bass.ds(tok * NT + t, 1)], xt,
                                                             ALU.mult, ALU.add)
                    ins.then_inc(s_res, 1)
                else:
                    nc.vector.tensor_tensor(blk(tok), gated[:], blk(tok), ALU.add).then_inc(s_res, 1)

            def shift_scale_rows(f):
                rows = (ps_h[:, 0, :], ps_o[:, 0:2, :].rearrange("p t d -> p (t d)"))[f]
                dve.wait_ge(s_adab[f], 16)
                dve.wait_ge(s_emb, f + 1)
                nc.vector.scalar_tensor_tensor(scale1[f][:], rows[:, D:2 * D], 1.0, adab[:, f, D:2 * D],
                                               ALU.add, ALU.add).then_inc(s_rows, 1)
                nc.vector.tensor_tensor(shift[f][:], rows[:, 0:D], adab[:, f, 0:D], ALU.add).then_inc(s_rows, 1)

            def gate_rows():
                dve.wait_ge(s_emb, 3)
                for f in range(2):
                    nc.vector.tensor_tensor(gate[f][:], ps_o[:, 2 + f, :], adab[:, f, 2 * D:3 * D],
                                            ALU.add).then_inc(s_gate, 1)
                dve.wait_ge(s_b2, 16)
                nc.vector.tensor_tensor(b2s[:, 0, :], b2s[:, 0, :], b2s[:, 1, :],
                                        ALU.add).then_inc(s_gate, 1)
                dve.wait_ge(s_gate, 3)
                for f in range(2):
                    nc.vector.tensor_tensor(gateb[f][:], b2s[:, 2 * f, :], gate[f][:],
                                            ALU.mult).then_inc(s_gateb, 1)

            def step(i, q, fprev, fnext, first=False, second=False, last=False, tail=False):
                if not tail:
                    tile_stats(i + 2, fnext, q)
                    dve.wait_ge(s_stat, i + 3)
                if first:
                    g_low(i, q, 0)
                elif second:
                    g_low(i, q, 0)
                else:
                    residual(i - 2, fprev[0])
                    g_low(i, q, 0)
                if not tail:
                    variance(i + 2, q)
                g_low(i, q, 1)
                if not tail:
                    neg_mean_rstd(i + 2, q)
                if not last:
                    n_low(i + 1, 1 - q)
                if not first:
                    gate_half(i - 1, fprev[1], 0, first=second)
                if not tail:
                    scale_rows(i + 2, fnext)
                g_low(i, q, 2)
                g_low(i, q, 3)
                if not first:
                    gate_half(i - 1, fprev[1], 1)

            last_x = X[:, (NB - 1) * BW:NB * BW].rearrange("p (t d) -> p t d", d=D)

            def first_variance(b, q):
                tile_stats(b, 0, q, first=True)
                dve.wait_ge(s_stat, b + 1)
                variance(b, q)

            dve.wait_ge(s_tanh, 1)
            nc.vector.tensor_scalar(th[:], th[:], 1.0, 0.5, ALU.add, ALU.mult).then_inc(s_th1, 1)
            dve.wait_ge(s_th1, 1)
            nc.vector.tensor_tensor(silu[:].rearrange("p k (b r) -> p (k b) r", r=P // B),
                                    th[:].rearrange("p k b -> p (k b)").unsqueeze(2).broadcast_to([P, KD * B, P // B]),
                                    ct[:].rearrange("p k b -> p (k b)").unsqueeze(2).broadcast_to([P, KD * B, P // B]),
                                    ALU.mult).then_inc(s_silu, 1)
            first_variance(0, 0)
            dve.wait_ge(s_rstd, 1)
            first_variance(1, 1)
            neg_mean_rstd(0, 0)
            dve.wait_ge(s_nmr, 1)
            for t in range(NT):
                ins = nc.vector.tensor_scalar(norm[:, t * D:(t + 1) * D], X[:, t * D:(t + 1) * D],
                                              rstd[0][:, t:t + 1], nmr[0][:, t:t + 1], ALU.mult, ALU.add)
            ins.then_inc(s_norm0, 1)
            neg_mean_rstd(1, 1)
            shift_scale_rows(0)
            dve.wait_ge(s_rows, 2)
            dve.wait_ge(s_norm0, 1)
            halves = [norm[:, 2 * j * D:(2 * j + 2) * D].rearrange("p (t d) -> p t d", d=D) for j in range(2)]
            for half in halves:
                nc.vector.tensor_tensor(half, half, scale1[0][:].unsqueeze(1).broadcast_to([P, 2, D]),
                                        ALU.mult).then_inc(s_norm0, 1)
            for j, half in enumerate(halves):
                dve.wait_ge(s_norm0, j + 2)
                ins = nc.vector.tensor_tensor(half, half, shift[0][:].unsqueeze(1).broadcast_to([P, 2, D]),
                                              ALU.add)
                ins.then_inc(s_norm, 1) if j else ins.then_inc(s_half0, 1)
            n_low(0, 0)
            scale_rows(1, 0)
            dve.wait_ge(s_maskl, 16)
            nc.vector.tensor_copy(maskf[:], mask8[:]).then_inc(s_mask, 1)
            step(0, 0, (0, 0), 0, first=True)
            shift_scale_rows(1)
            gate_rows()
            dve.wait_ge(s_gateb, 2)
            dve.wait_ge(s_rows, 4)
            dve.wait_ge(s_mask, 1)
            step(1, 1, (0, 0), 0, second=True)
            step(2, 0, (0, 0), 0)
            with dve.Fori(1, PAIRS - 1) as k:
                step(2 * k + 1, 1, (0, 0), 0)
                step(2 * k + 2, 0, (0, 0), 0)
            step(NB - 3, 1, (0, 0), 0)
            step(NB - 2, 0, (0, 0), 1)
            step(NB - 1, 1, (0, 0), 1)
            step(NB, 0, (0, 0), 1)
            step(NB + 1, 1, (0, 1), 1)
            step(NB + 2, 0, (1, 1), 1)
            with dve.Fori(1, PAIRS - 1) as k:
                step(2 * k + (NB + 1), 1, (1, 1), 1)
                step(2 * k + (NB + 2), 0, (1, 1), 1)
            step(ALL - 3, 1, (1, 1), 1)
            step(ALL - 2, 0, (1, 1), 1, tail=True)
            step(ALL - 1, 1, (1, 1), 1, tail=True, last=True)
            residual(ALL - 2, 1)
            nc.vector.tensor_tensor(last_x, last_x, gateb[1][:].unsqueeze(1).broadcast_to([P, NT, D]),
                                    ALU.add).then_inc(s_pre, 1)
            for j in range(2):
                gate_half(ALL - 1, 1, j)
                dve.wait_ge(s_pre, 1)
                dve.wait_ge(s_gated, 2 * (ALL - 1) + (j + 1))
                xh = X[:, (NB - 1) * BW + 2 * j * D:(NB - 1) * BW + (2 * j + 2) * D]
                nc.vector.tensor_tensor(xh, gated[:, 2 * j * D:(2 * j + 2) * D], xh,
                                        ALU.add).then_inc(s_tail, 1)

        @block.tensor
        def _(pe):
            def embed(dst, f, lo, hi, loaded):
                pe.wait_ge(loaded, 16)
                for k in range(KD):
                    last = nc.tensor.matmul(dst, silu[:, k, :], adaw[f][:, k, lo:hi],
                                            start=(k == 0), stop=(k == KD - 1))
                return last

            def keep_warm(n):
                for _ in range(n):
                    nc.tensor.matmul(ps_o[:, 0:2, :].rearrange("p t d -> p (t d)"), warm[:, 0:P], warm[:],
                                     start=True, stop=True)

            def transposes(b, first=False):
                if first:
                    pe.wait_ge(s_half0, 1)
                else:
                    pe.wait_ge(s_norm, b + 1)
                if not first:
                    pe.wait_ge(s_nlo, KD * b)
                for t in range(NT):
                    if first and t == NT // 2:
                        pe.wait_ge(s_norm, 1)
                    for k in range(KD):
                        last = nc.tensor.transpose(ps_n[:, k, t * P:(t + 1) * P],
                                                   norm[:, t * D + k * P:t * D + (k + 1) * P], ident[:])
                last.then_inc(s_T, 1)

            def first_product(i, q, f, c, first=False):
                if not first:
                    pe.wait_ge(s_glo, HC * i + (c + 1 - HC))
                terms = [(w, n, k) for n in (n_hi[q], n_lo[q]) for k in range(KD) for w in (w1_hi[f], w1_lo[f])
                         if n is n_hi[q] or w is w1_hi[f]]
                for m, (w, n, k) in enumerate(terms):
                    if c == 0 and w is w1_hi[f]:
                        pe.wait_ge(s_nhi if n is n_hi[q] else s_nlo, KD * i + (k + 1))
                    last = nc.tensor.matmul(ps_h[:, c, :], w[:, k, c * P:(c + 1) * P], n[:, k, :],
                                            start=(m == 0), stop=(m == len(terms) - 1))
                last.then_inc(s_h, 1)

            def second_product(b, q, f, t, first=False):
                if t == 0:
                    pe.wait_ge(s_glo, HC * b + HC)
                if t % 2 == 0 and not first:
                    pe.wait_ge(s_gated, 2 * b + (t // 2 - 1))
                elif t == 0:
                    pe.wait_ge(s_rows, 4)
                elif t == 2:
                    pe.wait_ge(s_gate, 2)
                for c in range(HC):
                    for n, (g, w) in enumerate(((g_hi[q], w2_hi[f]), (g_hi[q], w2_lo[f]), (g_lo[q], w2_hi[f]))):
                        last = nc.tensor.matmul(ps_o[:, t, :], g[:, c, t * P:(t + 1) * P], w[:, c, :],
                                                start=(c == 0 and n == 0), stop=(c == HC - 1 and n == 2))
                if t % 2 == 1:
                    last.then_inc(s_o, 1)

            def step(i, q, f, fprev, first=False, second=False, last=False):
                for c in range(HC):
                    first_product(i, q, f, c, first)
                    if c == (2 if first else 1) and not last:
                        transposes(i + 1)
                    if not first:
                        second_product(i - 1, 1 - q, fprev, c, first=second)

            pe.wait_ge(s_warm, 1)
            keep_warm(WARM[0])
            pe.wait_ge(s_silu, 1)
            embed(ps_h[:, 0, :], 0, 0, 2 * D, s_ada[0]).then_inc(s_emb, 1)
            pe.wait_ge(s_id, 1)
            keep_warm(WARM[1])
            transposes(0, first=True)
            keep_warm(WARM[2])
            pe.wait_ge(s_rows, 2)
            pe.wait_ge(s_wsplit, 1)
            step(0, 0, 0, 0, first=True)
            embed(ps_o[:, 0:2, :].rearrange("p t d -> p (t d)"), 1, 0, 2 * D, s_ada[1]).then_inc(s_emb, 1)
            embed(ps_o[:, 2, :], 0, 2 * D, 3 * D, s_adag[0])
            embed(ps_o[:, 3, :], 1, 2 * D, 3 * D, s_adag[1]).then_inc(s_emb, 1)
            pe.wait_ge(s_wsplit, 2)
            step(1, 1, 0, 0, second=True)
            step(2, 0, 0, 0)
            with pe.Fori(1, PAIRS) as k:
                step(2 * k + 1, 1, 0, 0)
                step(2 * k + 2, 0, 0, 0)
            step(NB - 1, 1, 0, 0)
            pe.wait_ge(s_wsplit, 3)
            step(NB, 0, 1, 0)
            pe.wait_ge(s_wsplit, 4)
            with pe.Fori(0, PAIRS) as k:
                step(2 * k + (NB + 1), 1, 1, 1)
                step(2 * k + (NB + 2), 0, 1, 1)
            step(ALL - 1, 1, 1, 1, last=True)
            for t in range(NT):
                second_product(ALL - 1, 1, 1, t)


def kernel(**inputs):
    import numpy as np
    import concourse.bacc as bacc
    from concourse import mybir as my
    from concourse.bass_utils import run_bass_kernel_spmd

    a = {k: np.asarray(v) for k, v in inputs.items()}
    L = "L0_cond_"
    cols = lambda v: v.reshape(-1, 128).T
    arrays = {
        "x": a["x"].reshape(128, -1),
        "condT": a["cond_1024"].T,
        "mask": a["mask_BxS_bk0"].reshape(128, -1),
        "ada_w": a[L + "ada_w"], "ada_b": a[L + "ada_b"].reshape(1, -1),
        "ssm_w1": a[L + "ssm_w1"], "ssm_w2": a[L + "ssm_w2"],
        "bwd_w1": a[L + "bwd_w1"], "bwd_w2": a[L + "bwd_w2"],
        "b1": np.concatenate([cols(a[L + n]) for n in ("ssm_b1", "bwd_b1", "ff_b1")], axis=1),
        "b2": np.stack([a[L + n] for n in ("ssm_b2", "bwd_b2", "ff_b2")])[None],
        "ffada_w": a[L + "ffada_w"], "ffada_b": a[L + "ffada_b"].reshape(1, -1),
        "ff_w1": a[L + "ff_w1"], "ff_w2": a[L + "ff_w2"],
    }
    arrays = {k: np.ascontiguousarray(v) for k, v in arrays.items()}
    nc = bacc.Bacc("TRN2", target_bir_lowering=False, num_devices=1)
    args = [nc.dram_tensor(k, v.shape, my.dt.from_np(v.dtype), kind="ExternalInput").ap()
            for k, v in arrays.items()]
    out = nc.dram_tensor("y", arrays["x"].shape, my.dt.float32, kind="ExternalOutput").ap()
    build(nc, *args, out)
    r = run_bass_kernel_spmd(nc, [arrays], core_ids=[0])
    return r.results[0]["y"].reshape(a["x"].shape)
```

```python
from contextlib import ExitStack

import concourse.bass as bass
from concourse import mybir

ALU = mybir.AluOpType
ACT = mybir.ActivationFunctionType
F32 = mybir.dt.float32
F32R = mybir.dt.float32r
U8 = mybir.dt.uint8

P = 128
D = 256
KD = D // P
H = 512
HC = H // P
NT = 4
BT = NT * P
BW = NT * D
EPS = 1e-6
HEAD = 2
PARTS = ((0, 2), (2, 1), (3, 1))
WARM = (12, 8, 1)


def build(nc, x, condT, mask, ada_w, ada_b, ssm_w1, ssm_w2, bwd_w1, bwd_w2, b1, b2, ffada_w, ffada_b,
          ff_w1, ff_w2, out):
    TILES = x.shape[1] // D
    NB = TILES // NT
    ALL = 2 * NB
    PAIRS = (NB - 2) // 2
    B = condT.shape[1]

    with ExitStack() as ctx:
        def sb(name, shape, dt=F32):
            return ctx.enter_context(nc.sbuf_tensor(name, shape, dt))

        def sem(name):
            return ctx.enter_context(nc.semaphore(name))

        X = sb("X", [P, TILES * D])
        xhat = sb("xhat", [P, BW])
        norm = sb("norm", [P, BW])
        n_hi = [sb(f"n_hi{q}", [P, KD, BT], F32R) for q in range(2)]
        n_lo = [sb(f"n_lo{q}", [P, KD, BT], F32R) for q in range(2)]
        g_hi = [sb(f"g_hi{q}", [P, HC, BT], F32R) for q in range(2)]
        g_lo = [sb(f"g_lo{q}", [P, HC, BT], F32R) for q in range(2)]
        gated = sb("gated", [P, BW])
        w1 = [sb(f"w1_{f}", [P, KD, H]) for f in range(2)]
        w1_hi = [sb(f"w1_hi{f}", [P, KD, H], F32R) for f in range(2)]
        w1_lo = [sb(f"w1_lo{f}", [P, KD, H], F32R) for f in range(2)]
        w2 = [sb(f"w2_{f}", [P, HC, D]) for f in range(2)]
        w2_hi = [sb(f"w2_hi{f}", [P, HC, D], F32R) for f in range(2)]
        w2_lo = [sb(f"w2_lo{f}", [P, HC, D], F32R) for f in range(2)]
        adaw = [sb(f"adaw{f}", [P, KD, 3 * D]) for f in range(2)]
        adab = sb("adab", [P, 2, 3 * D])
        b2s = sb("b2s", [P, 3, D])
        b1s = sb("b1s", [P, 2 * HC])
        ct = sb("ct", [P, KD, B])
        th = sb("th", [P, KD, B])
        silu = sb("silu", [P, KD, P])
        warm = sb("warm", [P, BT], mybir.dt.bfloat16)
        ident = sb("ident", [P, P])
        shift = [sb(f"shift{f}", [P, D]) for f in range(2)]
        scale1 = [sb(f"scale1_{f}", [P, D]) for f in range(2)]
        gate = [sb(f"gate{f}", [P, D]) for f in range(2)]
        gateb = [sb(f"gateb{f}", [P, D]) for f in range(2)]
        mask8 = sb("mask8", [P, TILES], U8)
        maskf = sb("maskf", [P, TILES])
        table = sb("table", [P, 1])
        stats = sb("stats", [P, NT, 6])
        mv = [sb(f"mv{q}", [P, NT, 2]) for q in range(2)]
        nmr = [sb(f"nmr{q}", [P, NT]) for q in range(2)]
        vare = sb("vare", [P, NT])
        mhalf = sb("mhalf", [P, NT])
        rstd = [sb(f"rstd{q}", [P, NT]) for q in range(2)]

        ps_n = ctx.enter_context(nc.psum_tensor("ps_n", [P, KD, BT], F32))
        ps_h = ctx.enter_context(nc.psum_tensor("ps_h", [P, HC, BT], F32))
        ps_o = ctx.enter_context(nc.psum_tensor("ps_o", [P, NT, D], F32))

        s_cond = sem("cond_loaded")
        s_ada = [sem(f"ada_loaded{f}") for f in range(2)]
        s_ada0 = sem("ada_shift_loaded")
        s_adag = [sem(f"ada_gate_loaded{f}") for f in range(2)]
        s_bias = sem("b1_loaded")
        s_adab = [sem(f"ada_b_loaded{f}") for f in range(2)]
        s_adabg = sem("ada_b_gate_loaded")
        s_b2 = sem("b2_loaded")
        s_maskl = sem("mask_loaded")
        s_w1l = [[sem(f"w1_loaded{f}_{h}") for h in range(2)] for f in range(2)]
        s_w2l = [[sem(f"w2_loaded{f}_{h}") for h in range(2)] for f in range(2)]
        s_x0 = [sem(f"x0_half_loaded{j}") for j in range(2)]
        s_x = [sem(f"x_loaded{q}") for q in range(2)]
        s_const = sem("exponent_set")
        s_warm = sem("warm_set")
        s_id0 = sem("ident_zeroed")
        s_id = sem("ident_ready")
        s_tanh = sem("tanh_ready")
        s_th1 = sem("tanh_plus_one")
        s_silu = sem("silu_ready")
        s_emb = sem("emb_ready")
        s_scale = sem("scale_rows_ready")
        s_shift = sem("shift_rows_ready")
        s_gate = sem("gate_ready")
        s_b2sum = sem("b2_summed")
        s_gateb = sem("gateb_ready")
        s_mask = sem("maskf_ready")
        s_wsplit_hi = sem("weights_hi_ready")
        s_wsplit = sem("weights_split")
        s_var = sem("variance_ready")
        s_stat = sem("stats_ready")
        s_aggr = sem("mean_variance_ready")
        s_rstd = sem("rstd_ready")
        s_nmr = sem("nmr_ready")
        s_xhat = sem("xhat_ready")
        s_scaled = sem("scaled_ready")
        s_norm = sem("norm_ready")
        s_xhead = sem("xhat_head_ready")
        s_xtail0 = sem("xhat0_tail_ready")
        s_scaled0 = [sem(f"scaled0_{e}_ready") for e in ("head", "tail")]
        s_head0 = sem("norm0_head_ready")
        s_T = sem("transposed")
        s_nhi = sem("n_hi_ready")
        s_nlo = sem("n_lo_ready")
        s_h = sem("hidden_ready")
        s_gelu = sem("gelu_ready")
        s_ghi = sem("g_hi_ready")
        s_glo = sem("g_lo_ready")
        s_o = sem("output_ready")
        s_gated = sem("gated_ready")
        s_upd = sem("update_ready")
        s_res = sem("block_done")
        s_pre = sem("last_bias_added")
        s_tail = sem("last_part_done")
        s_out = [sem(f"y_stored{q}") for q in range(2)]
        s_outp = [sem(f"last_part_stored{j}") for j in range(len(PARTS))]

        def embed_rows(f):
            return (ps_h[:, 0, 0:D], ps_h[:, 1, 0:D]) if f == 0 else (ps_o[:, 0, :], ps_o[:, 1, :])

        def weight_half(w, h):
            return w[:, :, h * D:(h + 1) * D] if w.shape[1] == KD else w[:, 2 * h:2 * h + 2, :]

        last_psum = (ps_o[:, 0:2, :], ps_o[:, 2:3, :], ps_n[:, 0:1, 0:D])

        block = ctx.enter_context(nc.Block())

        def blk(b):
            return X[:, bass.ds(b * BW, BW)]

        @block.sync
        def _(sp):
            def store(b, q):
                sp.wait_ge(s_res, b + (NB + 1))
                sp.dma_start(out[:, bass.ds(b * BW, BW)],
                             X[:, bass.ds(b * BW, BW)]).then_inc(s_out[q], 16)

            def load_x(b, q):
                sp.dma_start(X[:, bass.ds(b * BW, BW)], x[:, bass.ds(b * BW, BW)]).then_inc(s_x[q], 16)

            def load_ada(f, lo, hi, w, loaded):
                sp.dma_start(adaw[f][:, :, lo:hi],
                             w[:, lo:hi].rearrange("(k p) n -> p k n", p=P)).then_inc(loaded, 16)

            for j in range(2):
                half = slice(2 * j * D, (2 * j + 2) * D)
                sp.dma_start(X[:, half], x[:, half]).then_inc(s_x0[j], 16)
            sp.dma_start(ct[:], condT.rearrange("(k p) b -> p k b", p=P)).then_inc(s_cond, 16)
            load_ada(0, D, 2 * D, ada_w, s_ada[0])
            load_ada(0, 0, D, ada_w, s_ada0)
            sp.dma_start(adab[:, 0, 0:2 * D], ada_b[:, 0:2 * D].broadcast_to([P, 2 * D])).then_inc(s_adab[0], 16)
            load_x(1, 1)
            for h, w in enumerate((ssm_w1, bwd_w1)):
                sp.dma_start(weight_half(w1[0], h), w.rearrange("(k p) n -> p k n", p=P)).then_inc(s_w1l[0][h], 16)
            for h, w in enumerate((ssm_w2, bwd_w2)):
                sp.dma_start(weight_half(w2[0], h), w.rearrange("(k p) n -> p k n", p=P)).then_inc(s_w2l[0][h], 16)
            sp.dma_start(b1s[:], b1).then_inc(s_bias, 16)
            load_x(2, 0)
            sp.dma_start(mask8[:], mask).then_inc(s_maskl, 16)
            load_ada(1, 0, 2 * D, ffada_w, s_ada[1])
            load_ada(0, 2 * D, 3 * D, ada_w, s_adag[0])
            load_ada(1, 2 * D, 3 * D, ffada_w, s_adag[1])
            sp.dma_start(adab[:, 1, :], ffada_b.broadcast_to([P, 3 * D])).then_inc(s_adab[1], 16)
            sp.dma_start(adab[:, 0, 2 * D:], ada_b[:, 2 * D:].broadcast_to([P, D])).then_inc(s_adabg, 16)
            sp.dma_start(b2s[:], b2.broadcast_to([P, 3, D])).then_inc(s_b2, 16)
            sp.wait_ge(s_x[1], 16)
            load_x(3, 1)
            with sp.Fori(2, NB // 2) as k:
                for q in range(2):
                    sp.wait_ge(s_x[q], 16 * k + (16 * q - 16))
                    load_x(2 * k + q, q)
            for w, src, loaded in ((w1[1], ff_w1, s_w1l[1]), (w2[1], ff_w2, s_w2l[1])):
                for h in range(2):
                    sp.dma_start(weight_half(w, h),
                                 weight_half(src.rearrange("(k p) n -> p k n", p=P), h)).then_inc(loaded[h], 16)
            with sp.Fori(0, NB // 2 - 1) as k:
                for q in range(2):
                    store(2 * k + q, q)
            store(NB - 2, 0)
            for j, (t, n) in enumerate(PARTS):
                part = slice((NB - 1) * BW + t * D, (NB - 1) * BW + (t + n) * D)
                sp.wait_ge(s_tail, j + 1)
                sp.dma_start(out[:, part], X[:, part]).then_inc(s_outp[j], 16)
            sp.wait_ge(s_out[0], 16 * (NB // 2))
            sp.wait_ge(s_out[1], 16 * (NB // 2 - 1))
            for j in range(len(PARTS)):
                sp.wait_ge(s_outp[j], 16)

        @block.gpsimd
        def _(pool):
            nc.gpsimd.memset(mhalf[:], -0.5).then_inc(s_const, 1)
            nc.gpsimd.memset(ident[:], 0.0).then_inc(s_id0, 1)
            pool.wait_ge(s_id0, 1)
            nc.gpsimd.affine_select(out=ident[:], in_=ident[:], compare_op=ALU.not_equal, fill=1.0, base=0,
                                    pattern=[[-1, P]], channel_multiplier=1).then_inc(s_id, 1)

            def reciprocal_std(b, q):
                pool.wait_ge(s_var, b + 1)
                nc.gpsimd.tensor_tensor(rstd[q][:], vare[:], mhalf[:], ALU.pow).then_inc(s_rstd, 1)

            def add_bias(b, f, j):
                half = gated[:, 2 * j * D:(2 * j + 2) * D].rearrange("p (t d) -> p t d", d=D)
                pool.wait_ge(s_gated, 2 * b + (j + 1))
                nc.gpsimd.tensor_tensor(half, half, gateb[f][:].unsqueeze(1).broadcast_to([P, 2, D]),
                                        ALU.add).then_inc(s_upd, 1)

            def add_shift(b, f):
                nt = norm[:].rearrange("p (t d) -> p t d", d=D)
                pool.wait_ge(s_scaled, b)
                nc.gpsimd.tensor_tensor(nt, nt, shift[f][:].unsqueeze(1).broadcast_to([P, NT, D]),
                                        ALU.add).then_inc(s_norm, 1)

            def split_lo(lo, src, hi, h, n):
                pool.wait_ge(s_wsplit_hi, n)
                nc.gpsimd.tensor_tensor(weight_half(lo, h), weight_half(src, h), weight_half(hi, h).bitcast(F32),
                                        ALU.subtract).then_inc(s_wsplit, 1)

            pool.wait_ge(s_const, 1)
            reciprocal_std(0, 0)
            part = norm[:, HEAD * D:NT * D].rearrange("p (t d) -> p t d", d=D)
            pool.wait_ge(s_scale, 1)
            pool.wait_ge(s_xtail0, 1)
            nc.gpsimd.tensor_tensor(part, part, scale1[0][:].unsqueeze(1).broadcast_to([P, NT - HEAD, D]),
                                    ALU.mult).then_inc(s_scaled0[1], 1)
            pool.wait_ge(s_shift, 1)
            pool.wait_ge(s_scaled0[1], 1)
            nc.gpsimd.tensor_tensor(part, part, shift[0][:].unsqueeze(1).broadcast_to([P, NT - HEAD, D]),
                                    ALU.add).then_inc(s_norm, 1)
            split_lo(w1_lo[0], w1[0], w1_hi[0], 0, 1)
            reciprocal_std(1, 1)
            split_lo(w1_lo[0], w1[0], w1_hi[0], 1, 2)
            split_lo(w2_lo[0], w2[0], w2_hi[0], 0, 3)
            add_shift(1, 0)

            def step(i, q, fprev, fnext, second=False, tail=False, split=None):
                if not second:
                    add_bias(i - 2, fprev[0], 1)
                if split:
                    for h in range(2):
                        split_lo(*split[:3], h, split[3] + h)
                if not tail:
                    reciprocal_std(i + 2, q)
                add_bias(i - 1, fprev[1], 0)
                if not tail:
                    add_shift(i + 2, fnext)

            reciprocal_std(2, 0)
            split_lo(w2_lo[0], w2[0], w2_hi[0], 1, 4)
            add_shift(2, 0)
            pool.wait_ge(s_b2, 16)
            nc.gpsimd.tensor_tensor(b2s[:, 0, :], b2s[:, 0, :], b2s[:, 1, :],
                                    ALU.add).then_inc(s_b2sum, 1)
            pool.wait_ge(s_b2sum, 1)
            pool.wait_ge(s_gate, 2)
            for f in range(2):
                nc.gpsimd.tensor_tensor(gateb[f][:], b2s[:, 2 * f, :], gate[f][:],
                                        ALU.mult).then_inc(s_gateb, 1)
            pool.wait_ge(s_gateb, 2)
            step(1, 1, (0, 0), 0, second=True)
            step(2, 0, (0, 0), 0)
            with pool.Fori(1, PAIRS - 1) as k:
                step(2 * k + 1, 1, (0, 0), 0)
                step(2 * k + 2, 0, (0, 0), 0)
            step(NB - 3, 1, (0, 0), 0)
            step(NB - 2, 0, (0, 0), 1, split=(w1_lo[1], w1[1], w1_hi[1], 5))
            step(NB - 1, 1, (0, 0), 1, split=(w2_lo[1], w2[1], w2_hi[1], 7))
            step(NB, 0, (0, 0), 1)
            step(NB + 1, 1, (0, 1), 1)
            step(NB + 2, 0, (1, 1), 1)
            with pool.Fori(1, PAIRS - 1) as k:
                step(2 * k + (NB + 1), 1, (1, 1), 1)
                step(2 * k + (NB + 2), 0, (1, 1), 1)
            step(ALL - 3, 1, (1, 1), 1)
            step(ALL - 2, 0, (1, 1), 1, tail=True)
            add_bias(ALL - 3, 1, 1)
            last_x = X[:, (NB - 1) * BW:NB * BW].rearrange("p (t d) -> p t d", d=D)
            pool.wait_ge(s_xhat, ALL - 1)
            nc.gpsimd.tensor_tensor(last_x, last_x, gateb[1][:].unsqueeze(1).broadcast_to([P, NT, D]),
                                    ALU.add).then_inc(s_pre, 1)
            add_bias(ALL - 2, 1, 0)
            add_bias(ALL - 2, 1, 1)

        @block.scalar
        def _(act):
            act.wait_ge(s_cond, 16)
            nc.scalar.activation(th[:], ct[:], ACT.Tanh, scale=0.5).then_inc(s_tanh, 1)
            act.wait_ge(s_const, 1)
            nc.scalar.activation(table[:], mhalf[:, 0:1], ACT.Gelu)

            def split_hi(dst, src, loaded, h):
                act.wait_ge(loaded[h], 16)
                nc.scalar.activation(weight_half(dst, h), weight_half(src, h), ACT.Copy).then_inc(s_wsplit_hi, 1)

            def normalise(b, q, f, dst, tiles, done):
                tok = b - NB * f
                act.wait_ge(s_nmr, b + 1)
                for t in tiles:
                    ins = nc.scalar.activation(dst[:, t * D:(t + 1) * D], X[:, bass.ds(tok * BW + t * D, D)],
                                               ACT.Identity, bias=nmr[q][:, t:t + 1], scale=rstd[q][:, t:t + 1])
                ins.then_inc(done, 1)

            def n_high(b, q):
                act.wait_ge(s_T, b + 1)
                for k in range(KD):
                    nc.scalar.activation(n_hi[q][:, k, :], ps_n[:, k, :], ACT.Copy).then_inc(s_nhi, 1)

            def gelu(i, q, f, c):
                func = (ACT.Gelu, ACT.Gelu_apprx_tanh)[f]
                act.wait_ge(s_h, HC * i + (c + 1))
                nc.scalar.activation(ps_h[:, c, :], ps_h[:, c, :], func,
                                     bias=b1s[:, f * HC + c:f * HC + c + 1]).then_inc(s_gelu, 1)
                act.wait_ge(s_gelu, HC * i + (c + 1))
                nc.scalar.activation(g_hi[q][:, c, :], ps_h[:, c, :], ACT.Copy).then_inc(s_ghi, 1)

            def step(i, q, f, fnext, second=False, last=False, tail=False, split=None):
                gelu(i, q, f, 0)
                gelu(i, q, f, 1)
                if second:
                    gelu(i, q, f, 2)
                if not last:
                    n_high(i + 1, 1 - q)
                if split:
                    for h in range(2):
                        split_hi(*split, h)
                if not tail:
                    act.wait_ge(s_scaled, i + 1)
                    normalise(i + 2, q, fnext, xhat, range(NT), s_xhat)
                if not second:
                    gelu(i, q, f, 2)
                gelu(i, q, f, 3)

            normalise(0, 0, 0, norm, (2, 3), s_xtail0)
            split_hi(w1_hi[0], w1[0], s_w1l[0], 0)
            split_hi(w1_hi[0], w1[0], s_w1l[0], 1)
            n_high(0, 0)
            split_hi(w2_hi[0], w2[0], s_w2l[0], 0)
            normalise(1, 1, 0, xhat, (2, 3), s_xhat)
            act.wait_ge(s_bias, 16)
            gelu(0, 0, 0, 0)
            gelu(0, 0, 0, 1)
            split_hi(w2_hi[0], w2[0], s_w2l[0], 1)
            gelu(0, 0, 0, 2)
            gelu(0, 0, 0, 3)
            n_high(1, 1)
            act.wait_ge(s_scaled, 1)
            normalise(2, 0, 0, xhat, range(NT), s_xhat)
            step(1, 1, 0, 0, second=True)
            step(2, 0, 0, 0)
            with act.Fori(1, PAIRS - 1) as k:
                step(2 * k + 1, 1, 0, 0)
                step(2 * k + 2, 0, 0, 0)
            step(NB - 3, 1, 0, 0, split=(w1_hi[1], w1[1], s_w1l[1]))
            step(NB - 2, 0, 0, 1, split=(w2_hi[1], w2[1], s_w2l[1]))
            step(NB - 1, 1, 0, 1)
            step(NB, 0, 1, 1)
            with act.Fori(0, PAIRS - 1) as k:
                step(2 * k + (NB + 1), 1, 1, 1)
                step(2 * k + (NB + 2), 0, 1, 1)
            step(ALL - 3, 1, 1, 1)
            step(ALL - 2, 0, 1, 1, tail=True)
            step(ALL - 1, 1, 1, 1, tail=True, last=True)

        @block.vector
        def _(dve):
            def tile_stats(b, f, q, first=False):
                tok = b - NB * f
                if f == 1:
                    dve.wait_ge(s_res, b - (NB - 1))
                elif not first:
                    dve.wait_ge(s_x[q], 8 * b + 8 * q)
                for t in range(NT):
                    if first and t % 2 == 0:
                        dve.wait_ge(s_x0[t // 2], 16)
                    ins = nc.vector.bn_stats(stats[:, t, :], X[:, bass.ds(tok * BW + t * D, D)])
                ins.then_inc(s_stat, 1)

            def variance(b, q):
                for t in range(NT):
                    ins = nc.vector.bn_aggr(mv[q][:, t, :], stats[:, t, :])
                ins.then_inc(s_aggr, 1)
                dve.wait_ge(s_aggr, b + 1)
                nc.vector.tensor_scalar(vare[:], mv[q][:, :, 1], EPS, None, ALU.add).then_inc(s_var, 1)

            def neg_mean_rstd(b, q):
                dve.wait_ge(s_rstd, b + 1)
                nc.vector.scalar_tensor_tensor(nmr[q][:], mv[q][:, :, 0], -1.0, rstd[q][:],
                                               ALU.mult, ALU.mult).then_inc(s_nmr, 1)

            def scale_rows(b, f):
                dve.wait_ge(s_T, b)
                dve.wait_ge(s_xhat, b)
                return nc.vector.tensor_tensor(
                    norm[:].rearrange("p (t d) -> p t d", d=D), xhat[:].rearrange("p (t d) -> p t d", d=D),
                    scale1[f][:].unsqueeze(1).broadcast_to([P, NT, D]), ALU.mult).then_inc(s_scaled, 1)

            def n_low(b, q):
                for k in range(KD):
                    dve.wait_ge(s_nhi, KD * b + (k + 1))
                    nc.vector.tensor_tensor(n_lo[q][:, k, :], ps_n[:, k, :], n_hi[q][:, k, :].bitcast(F32),
                                            ALU.subtract).then_inc(s_nlo, 1)

            def g_low(i, q, c):
                dve.wait_ge(s_ghi, HC * i + (c + 1))
                nc.vector.tensor_tensor(g_lo[q][:, c, :], ps_h[:, c, :], g_hi[q][:, c, :].bitcast(F32),
                                        ALU.subtract).then_inc(s_glo, 1)

            def gate_half(b, f, j, first=False):
                if j == 0 and not first:
                    dve.wait_ge(s_res, b)
                dve.wait_ge(s_o, 2 * b + (j + 1))
                nc.vector.tensor_tensor(
                    gated[:, 2 * j * D:(2 * j + 2) * D].rearrange("p (t d) -> p t d", d=D),
                    ps_o[:, 2 * j:2 * j + 2, :], gate[f][:].unsqueeze(1).broadcast_to([P, 2, D]),
                    ALU.mult).then_inc(s_gated, 1)

            def residual(b, f):
                tok = b - NB * f
                dve.wait_ge(s_upd, 2 * b + 2)
                if f == 0:
                    for t in range(NT):
                        xt = X[:, bass.ds(tok * BW + t * D, D)]
                        ins = nc.vector.scalar_tensor_tensor(xt, gated[:, t * D:(t + 1) * D],
                                                             maskf[:, bass.ds(tok * NT + t, 1)], xt,
                                                             ALU.mult, ALU.add)
                    ins.then_inc(s_res, 1)
                else:
                    nc.vector.tensor_tensor(blk(tok), gated[:], blk(tok), ALU.add).then_inc(s_res, 1)

            def scale_row(f):
                dve.wait_ge(s_emb, 2 * f + 1)
                dve.wait_ge(s_adab[f], 16)
                nc.vector.scalar_tensor_tensor(scale1[f][:], embed_rows(f)[1], 1.0, adab[:, f, D:2 * D],
                                               ALU.add, ALU.add).then_inc(s_scale, 1)

            def shift_row(f):
                dve.wait_ge(s_emb, f + 2)
                nc.vector.tensor_tensor(shift[f][:], embed_rows(f)[0], adab[:, f, 0:D], ALU.add).then_inc(s_shift, 1)

            def normalise_head(b, dst):
                dve.wait_ge(s_nmr, b + 1)
                for t in range(2):
                    ins = nc.vector.tensor_scalar(dst[:, t * D:(t + 1) * D], X[:, b * BW + t * D:b * BW + (t + 1) * D],
                                                  rstd[b][:, t:t + 1], nmr[b][:, t:t + 1], ALU.mult, ALU.add)
                ins.then_inc(s_xhead, 1)

            def gate_rows():
                dve.wait_ge(s_emb, 4)
                dve.wait_ge(s_adabg, 16)
                for f in range(2):
                    nc.vector.tensor_tensor(gate[f][:], ps_o[:, 2 + f, :], adab[:, f, 2 * D:],
                                            ALU.add).then_inc(s_gate, 1)

            def step(i, q, fprev, fnext, second=False, last=False, tail=False):
                if not tail:
                    tile_stats(i + 2, fnext, q)
                    dve.wait_ge(s_stat, i + 3)
                g_low(i, q, 0)
                if not tail:
                    variance(i + 2, q)
                if not second:
                    residual(i - 2, fprev[0])
                g_low(i, q, 1)
                if not tail:
                    neg_mean_rstd(i + 2, q)
                if second:
                    g_low(i, q, 2)
                if not last:
                    n_low(i + 1, 1 - q)
                gate_half(i - 1, fprev[1], 0, first=second)
                if not tail:
                    scale_rows(i + 2, fnext)
                if not second:
                    g_low(i, q, 2)
                g_low(i, q, 3)
                gate_half(i - 1, fprev[1], 1)

            nc.vector.memset(warm[:], 0.0).then_inc(s_warm, 1)
            tile_stats(0, 0, 0, first=True)
            dve.wait_ge(s_stat, 1)
            variance(0, 0)
            dve.wait_ge(s_tanh, 1)
            nc.vector.tensor_scalar(th[:], th[:], 1.0, 0.5, ALU.add, ALU.mult).then_inc(s_th1, 1)
            dve.wait_ge(s_th1, 1)
            nc.vector.tensor_tensor(silu[:].rearrange("p k (b r) -> p (k b) r", r=P // B),
                                    th[:].rearrange("p k b -> p (k b)").unsqueeze(2).broadcast_to([P, KD * B, P // B]),
                                    ct[:].rearrange("p k b -> p (k b)").unsqueeze(2).broadcast_to([P, KD * B, P // B]),
                                    ALU.mult).then_inc(s_silu, 1)
            neg_mean_rstd(0, 0)
            normalise_head(0, norm)
            scale_row(0)
            part = norm[:, 0:HEAD * D].rearrange("p (t d) -> p t d", d=D)
            dve.wait_ge(s_scale, 1)
            dve.wait_ge(s_xhead, 1)
            nc.vector.tensor_tensor(part, part, scale1[0][:].unsqueeze(1).broadcast_to([P, HEAD, D]),
                                    ALU.mult).then_inc(s_scaled0[0], 1)
            shift_row(0)
            dve.wait_ge(s_shift, 1)
            dve.wait_ge(s_scaled0[0], 1)
            nc.vector.tensor_tensor(part, part, shift[0][:].unsqueeze(1).broadcast_to([P, HEAD, D]),
                                    ALU.add).then_inc(s_head0, 1)
            tile_stats(1, 0, 1)
            dve.wait_ge(s_stat, 2)
            variance(1, 1)
            n_low(0, 0)
            neg_mean_rstd(1, 1)
            normalise_head(1, xhat)
            dve.wait_ge(s_xhead, 2)
            scale_rows(1, 0)
            tile_stats(2, 0, 0)
            dve.wait_ge(s_stat, 3)
            g_low(0, 0, 0)
            variance(2, 0)
            g_low(0, 0, 1)
            g_low(0, 0, 2)
            neg_mean_rstd(2, 0)
            g_low(0, 0, 3)
            scale_row(1)
            shift_row(1)
            n_low(1, 1)
            scale_rows(2, 0)
            dve.wait_ge(s_maskl, 16)
            nc.vector.tensor_copy(maskf[:], mask8[:]).then_inc(s_mask, 1)
            gate_rows()
            dve.wait_ge(s_gate, 2)
            dve.wait_ge(s_scale, 2)
            dve.wait_ge(s_mask, 1)
            step(1, 1, (0, 0), 0, second=True)
            step(2, 0, (0, 0), 0)
            with dve.Fori(1, PAIRS - 1) as k:
                step(2 * k + 1, 1, (0, 0), 0)
                step(2 * k + 2, 0, (0, 0), 0)
            step(NB - 3, 1, (0, 0), 0)
            step(NB - 2, 0, (0, 0), 1)
            step(NB - 1, 1, (0, 0), 1)
            step(NB, 0, (0, 0), 1)
            step(NB + 1, 1, (0, 1), 1)
            step(NB + 2, 0, (1, 1), 1)
            with dve.Fori(1, PAIRS - 1) as k:
                step(2 * k + (NB + 1), 1, (1, 1), 1)
                step(2 * k + (NB + 2), 0, (1, 1), 1)
            step(ALL - 3, 1, (1, 1), 1)
            step(ALL - 2, 0, (1, 1), 1, tail=True)
            step(ALL - 1, 1, (1, 1), 1, tail=True, last=True)
            residual(ALL - 2, 1)
            for j, (t, n) in enumerate(PARTS):
                part = gated[:, t * D:(t + n) * D]
                if j == 0:
                    dve.wait_ge(s_res, ALL - 1)
                dve.wait_ge(s_o, 2 * (ALL - 1) + (j + 1))
                nc.vector.tensor_tensor(part.rearrange("p (t d) -> p t d", d=D), last_psum[j],
                                        gate[1][:].unsqueeze(1).broadcast_to([P, n, D]),
                                        ALU.mult).then_inc(s_gated, 1)
                dve.wait_ge(s_pre, 1)
                dve.wait_ge(s_gated, 2 * (ALL - 1) + (j + 1))
                xp = X[:, (NB - 1) * BW + t * D:(NB - 1) * BW + (t + n) * D]
                nc.vector.tensor_tensor(xp, part, xp, ALU.add).then_inc(s_tail, 1)

        @block.tensor
        def _(pe):
            def embed(dst, f, m, w_loaded):
                pe.wait_ge(w_loaded, 16)
                for k in range(KD):
                    ins = nc.tensor.matmul(dst, silu[:, k, :], adaw[f][:, k, m * D:(m + 1) * D],
                                           start=(k == 0), stop=(k == KD - 1))
                return ins

            def keep_warm(n):
                for _ in range(n):
                    nc.tensor.matmul(ps_o[:, 0:2, :].rearrange("p t d -> p (t d)"), warm[:, 0:P], warm[:],
                                     start=True, stop=True)

            def transposes(b, first=False):
                if first:
                    pe.wait_ge(s_head0, 1)
                else:
                    pe.wait_ge(s_norm, b + 1)
                if not first:
                    pe.wait_ge(s_nlo, KD * b)
                for t in range(NT):
                    if first and t == HEAD:
                        pe.wait_ge(s_norm, 1)
                    for k in range(KD):
                        last = nc.tensor.transpose(ps_n[:, k, t * P:(t + 1) * P],
                                                   norm[:, t * D + k * P:t * D + (k + 1) * P], ident[:])
                last.then_inc(s_T, 1)

            def first_product(i, q, f, c, first=False):
                if not first:
                    pe.wait_ge(s_glo, HC * i + (c + 1 - HC))
                terms = [(w, n, k) for n in (n_hi[q], n_lo[q]) for k in range(KD) for w in (w1_hi[f], w1_lo[f])
                         if n is n_hi[q] or w is w1_hi[f]]
                for m, (w, n, k) in enumerate(terms):
                    if c == 0 and w is w1_hi[f]:
                        pe.wait_ge(s_nhi if n is n_hi[q] else s_nlo, KD * i + (k + 1))
                    last = nc.tensor.matmul(ps_h[:, c, :], w[:, k, c * P:(c + 1) * P], n[:, k, :],
                                            start=(m == 0), stop=(m == len(terms) - 1))
                last.then_inc(s_h, 1)

            def second_product(b, q, f, t, first=False, last=False):
                if t == 0:
                    pe.wait_ge(s_glo, HC * b + HC)
                if t % 2 == 0 and not first:
                    pe.wait_ge(s_gated, 2 * b + (t // 2 - 1))
                elif t == 0:
                    pe.wait_ge(s_scale, 2)
                    pe.wait_ge(s_shift, 2)
                elif t == 2:
                    pe.wait_ge(s_gate, 2)
                dst = last_psum[2][:, 0, :] if last and t == 3 else ps_o[:, t, :]
                for c in range(HC):
                    if first and t == 0 and c % 2 == 0:
                        pe.wait_ge(s_wsplit, 3 + c // 2)
                    for n, (g, w) in enumerate(((g_hi[q], w2_hi[f]), (g_hi[q], w2_lo[f]), (g_lo[q], w2_hi[f]))):
                        ins = nc.tensor.matmul(dst, g[:, c, t * P:(t + 1) * P], w[:, c, :],
                                               start=(c == 0 and n == 0), stop=(c == HC - 1 and n == 2))
                if t % 2 == 1 or (last and t == 2):
                    ins.then_inc(s_o, 1)

            def step(i, q, f, fprev, second=False, last=False):
                tiles_after = ((0,), (1,), (), (2, 3)) if last else ((0,), (1,), (2,), (3,))
                for c in range(HC):
                    first_product(i, q, f, c)
                    if c == (2 if second else 1) and not last:
                        transposes(i + 1)
                    for t in tiles_after[c]:
                        second_product(i - 1, 1 - q, fprev, t, first=second)

            pe.wait_ge(s_warm, 1)
            keep_warm(WARM[0])
            pe.wait_ge(s_silu, 1)
            embed(embed_rows(0)[1], 0, 1, s_ada[0]).then_inc(s_emb, 1)
            embed(embed_rows(0)[0], 0, 0, s_ada0).then_inc(s_emb, 1)
            pe.wait_ge(s_id, 1)
            keep_warm(WARM[1])
            transposes(0, first=True)
            keep_warm(WARM[2])
            pe.wait_ge(s_scale, 1)
            pe.wait_ge(s_shift, 1)
            for c in range(HC):
                if c % 2 == 0:
                    pe.wait_ge(s_wsplit, 1 + c // 2)
                first_product(0, 0, 0, c, first=True)
            embed(embed_rows(1)[0], 1, 0, s_ada[1])
            embed(embed_rows(1)[1], 1, 1, s_ada[1]).then_inc(s_emb, 1)
            transposes(1)
            embed(ps_o[:, 2, :], 0, 2, s_adag[0])
            embed(ps_o[:, 3, :], 1, 2, s_adag[1]).then_inc(s_emb, 1)
            step(1, 1, 0, 0, second=True)
            step(2, 0, 0, 0)
            with pe.Fori(1, PAIRS) as k:
                step(2 * k + 1, 1, 0, 0)
                step(2 * k + 2, 0, 0, 0)
            step(NB - 1, 1, 0, 0)
            pe.wait_ge(s_wsplit, 6)
            step(NB, 0, 1, 0)
            pe.wait_ge(s_wsplit, 8)
            with pe.Fori(0, PAIRS) as k:
                step(2 * k + (NB + 1), 1, 1, 1)
                step(2 * k + (NB + 2), 0, 1, 1)
            step(ALL - 1, 1, 1, 1, last=True)
            for t in range(NT):
                second_product(ALL - 1, 1, 1, t, last=True)


def kernel(**inputs):
    import numpy as np
    import concourse.bacc as bacc
    from concourse import mybir as my
    from concourse.bass_utils import run_bass_kernel_spmd

    a = {k: np.asarray(v) for k, v in inputs.items()}
    L = "L0_cond_"
    cols = lambda v: v.reshape(-1, 128).T
    arrays = {
        "x": a["x"].reshape(128, -1),
        "condT": a["cond_1024"].T,
        "mask": a["mask_BxS_bk0"].reshape(128, -1),
        "ada_w": a[L + "ada_w"], "ada_b": a[L + "ada_b"].reshape(1, -1),
        "ssm_w1": a[L + "ssm_w1"], "ssm_w2": a[L + "ssm_w2"],
        "bwd_w1": a[L + "bwd_w1"], "bwd_w2": a[L + "bwd_w2"],
        "b1": np.concatenate([cols(a[L + n]) for n in ("ssm_b1", "bwd_b1", "ff_b1")], axis=1),
        "b2": np.stack([a[L + n] for n in ("ssm_b2", "bwd_b2", "ff_b2")])[None],
        "ffada_w": a[L + "ffada_w"], "ffada_b": a[L + "ffada_b"].reshape(1, -1),
        "ff_w1": a[L + "ff_w1"], "ff_w2": a[L + "ff_w2"],
    }
    arrays = {k: np.ascontiguousarray(v) for k, v in arrays.items()}
    nc = bacc.Bacc("TRN2", target_bir_lowering=False, num_devices=1)
    args = [nc.dram_tensor(k, v.shape, my.dt.from_np(v.dtype), kind="ExternalInput").ap()
            for k, v in arrays.items()]
    out = nc.dram_tensor("y", arrays["x"].shape, my.dt.float32, kind="ExternalOutput").ap()
    build(nc, *args, out)
    r = run_bass_kernel_spmd(nc, [arrays], core_ids=[0])
    return r.results[0]["y"].reshape(a["x"].shape)
```
